# Optimizing a Trainium2 kernel written in Bass

```python
import numpy as np
import jax
import jax.numpy as jnp

def _softmax(x, axis=-1):
    return jax.nn.softmax(x, axis=axis)

def _gelu(x):
    return jax.nn.gelu(x, approximate=True)

def _silu(x):
    return jax.nn.silu(x)

def _sigmoid(x):
    return jax.nn.sigmoid(x)

def _layernorm(x, axis=-1, eps=1e-05):
    m = jnp.mean(x, axis=axis, keepdims=True)
    v = jnp.var(x, axis=axis, keepdims=True)
    return (x - m) / jnp.sqrt(v + eps)

def _scatter_add(tgt, idx, src, axis=0):
    return tgt.at[idx].add(src)

def _segment_sum(src, seg, n):
    return jax.ops.segment_sum(src, seg, n)
kernel_name = 'mk_seq_preln_d1_jaxref_r4_f7f46e'

def setup_inputs(seed: int=0):
    np.random.seed(seed)
    _w = jnp.asarray

    def _L0_attn_setup():
        import jax, jax.numpy as jnp
        import numpy as np
        B, S, D, N = (16, 512, 256, 16)
        key = jax.random.key(seed)
        ks = jax.random.split(key, 8)
        sc = lambda d: 1.0 / np.sqrt(d)
        return {'x': jax.random.normal(ks[0], (B, S, D), jnp.float32), 'WA': jax.random.normal(ks[1], (N, D), jnp.float32) * sc(D), 'WB': jax.random.normal(ks[2], (N, D), jnp.float32) * sc(D), 'WC': jax.random.normal(ks[3], (D, N), jnp.float32) * sc(N), 'WD': jax.random.normal(ks[4], (D, D), jnp.float32) * sc(D), 'bD': jax.random.normal(ks[5], (D,), jnp.float32) * 0.01, 'Wg': jax.random.normal(ks[6], (D, D), jnp.float32) * sc(D), 'bg': jax.random.normal(ks[7], (D,), jnp.float32) * 0.01}
    _L0_attn_in = _L0_attn_setup()

    def _L0_ffn_setup():
        import jax, jax.numpy as jnp
        import numpy as np
        B, S, H = (2, 512, 256)
        E, K, F_EXP, F_SHARED = (16, 2, 128, 256)
        key = jax.random.key(seed)
        ks = jax.random.split(key, 9)
        sc = 1.0 / np.sqrt(H)
        scf = 1.0 / np.sqrt(F_EXP)
        scfs = 1.0 / np.sqrt(F_SHARED)
        return {'x': jax.random.normal(ks[0], (B, S, H), dtype=jnp.float32), 'router_w': jax.random.normal(ks[1], (H, E), dtype=jnp.float32) * sc, 'gate_w': jax.random.normal(ks[2], (E, H, F_EXP), dtype=jnp.float32) * sc, 'up_w': jax.random.normal(ks[3], (E, H, F_EXP), dtype=jnp.float32) * sc, 'down_w': jax.random.normal(ks[4], (E, F_EXP, H), dtype=jnp.float32) * scf, 'shared_gate_w': jax.random.normal(ks[5], (H, F_SHARED), dtype=jnp.float32) * sc, 'shared_up_w': jax.random.normal(ks[6], (H, F_SHARED), dtype=jnp.float32) * sc, 'shared_down_w': jax.random.normal(ks[7], (F_SHARED, H), dtype=jnp.float32) * scfs}
    _L0_ffn_in = _L0_ffn_setup()
    _d = {'L0_attn_x': _L0_attn_in['x'], 'L0_attn_WA': _L0_attn_in['WA'], 'L0_attn_WB': _L0_attn_in['WB'], 'L0_attn_WC': _L0_attn_in['WC'], 'L0_attn_WD': _L0_attn_in['WD'], 'L0_attn_bD': _L0_attn_in['bD'], 'L0_attn_Wg': _L0_attn_in['Wg'], 'L0_attn_bg': _L0_attn_in['bg'], 'L0_ffn_router_w': _L0_ffn_in['router_w'], 'L0_ffn_gate_w': _L0_ffn_in['gate_w'], 'L0_ffn_up_w': _L0_ffn_in['up_w'], 'L0_ffn_down_w': _L0_ffn_in['down_w'], 'L0_ffn_shared_gate_w': _L0_ffn_in['shared_gate_w'], 'L0_ffn_shared_up_w': _L0_ffn_in['shared_up_w'], 'L0_ffn_shared_down_w': _L0_ffn_in['shared_down_w']}
    _x0 = _d['L0_attn_x']
    _d['L0_attn_x'] = jax.random.normal(jax.random.fold_in(jax.random.key(seed), 1), (16, 512, 256), dtype=_x0.dtype)
    del _x0
    return _d

def reference(L0_attn_x, L0_attn_WA, L0_attn_WB, L0_attn_WC, L0_attn_WD, L0_attn_bD, L0_attn_Wg, L0_attn_bg, L0_ffn_router_w, L0_ffn_gate_w, L0_ffn_up_w, L0_ffn_down_w, L0_ffn_shared_gate_w, L0_ffn_shared_up_w, L0_ffn_shared_down_w):

    def _L0_attn_ref(x, WA, WB, WC, WD, bD, Wg, bg):
        import jax, jax.numpy as jnp
        import numpy as np
        B, S, D, N = (16, 512, 256, 16)
        a = jnp.tanh(jnp.einsum('bsd,nd->bsn', x, WA))
        b = jnp.einsum('bsd,nd->bsn', x, WB)
        g = jax.nn.sigmoid(jnp.einsum('bsd,ed->bse', x, Wg) + bg)
        dx = jnp.einsum('bsd,ed->bse', x, WD) + bD

        def step(h, ab):
            a_t, b_t = ab
            h = a_t * h + b_t
            return (h, h)
        h0 = jnp.zeros((x.shape[0], WA.shape[0]), x.dtype)
        _, hs = jax.lax.scan(step, h0, (jnp.swapaxes(a, 0, 1), jnp.swapaxes(b, 0, 1)))
        hs = jnp.swapaxes(hs, 0, 1)
        y = jnp.einsum('bsn,en->bse', hs, WC) * g + dx * (1.0 - g)
        return y

    def _L0_ffn_ref(x, router_w, gate_w, up_w, down_w, shared_gate_w, shared_up_w, shared_down_w):
        import jax, jax.numpy as jnp
        import numpy as np
        B, S, H = (2, 512, 256)
        E, K, F_EXP, F_SHARED = (16, 2, 128, 256)
        b, s, h = x.shape
        T = b * s
        x_flat = x.reshape(T, h)
        shared_out = jax.nn.silu(x @ shared_gate_w) * (x @ shared_up_w) @ shared_down_w
        router_probs = jax.nn.softmax(x_flat @ router_w, axis=-1)
        topk_probs, topk_idx = jax.lax.top_k(router_probs, K)
        coeff = jnp.einsum('tk,tke->te', topk_probs, jax.nn.one_hot(topk_idx, E, dtype=x.dtype))

        def expert_step(acc, ws):
            g, u, d, c = ws
            inter = jax.nn.silu(x_flat @ g) * (x_flat @ u)
            return (acc + inter @ d * c[:, None], None)
        routed, _ = jax.lax.scan(expert_step, jnp.zeros((T, h), dtype=x.dtype), (gate_w, up_w, down_w, coeff.T))
        return routed.reshape(b, s, h) + shared_out
    x = L0_attn_x
    x = x + _L0_attn_ref(_layernorm(x, axis=-1), L0_attn_WA, L0_attn_WB, L0_attn_WC, L0_attn_WD, L0_attn_bD, L0_attn_Wg, L0_attn_bg)
    x = x + _L0_ffn_ref(_layernorm(x, axis=-1), L0_ffn_router_w, L0_ffn_gate_w, L0_ffn_up_w, L0_ffn_down_w, L0_ffn_shared_gate_w, L0_ffn_shared_up_w, L0_ffn_shared_down_w)
    return x

_drawn_inputs = setup_inputs


def setup_inputs(seed=0):
    import zlib

    import numpy as np

    out = dict(_drawn_inputs(seed))
    spreads = {}
    factors = {'L0_attn_bD': 7.758, 'L0_attn_bg': 8.0}
    for name, (base, spread) in spreads.items():
        noise = np.random.default_rng([zlib.crc32(name.encode()), seed]).standard_normal(out[name].shape)
        drawn = base * np.exp(spread * noise) if base else spread * noise
        out[name] = jnp.asarray(drawn.astype(out[name].dtype))
    for name, factor in factors.items():
        out[name] = (out[name] * factor).astype(out[name].dtype)
    return out
```

```python
from contextlib import ExitStack

import concourse.bass as bass
from concourse import mybir

ALU = mybir.AluOpType
ACT = mybir.ActivationFunctionType
AX_X = mybir.AxisListType.X
F32 = mybir.dt.float32
F32R = mybir.dt.float32r
BF16 = mybir.dt.bfloat16
I32 = mybir.dt.int32
U32 = mybir.dt.uint32

P = 128
EPS = 1e-5
RSQRT_SEED = 1597463007.0


def preln_gated_scan_and_routed_experts(nc, x, wa_t, wb_t, wc_t, wgd_t, bias, router_w, gate_w, up_w, down_w,
                                        shared_gu, shared_down, out):
    B, S, D = x.shape
    N = wa_t.shape[1]
    E = router_w.shape[1]
    F = gate_w.shape[2]
    TOP = 2
    T = B * S
    KC = D // P
    J = S // P
    NT = T // P
    TILES = TOP * NT + E
    PAIRS = TILES // 2
    REGION = T + P
    ROW = D + 4
    GU = KC * 2 * F
    NOWHERE = 2 ** 30
    W = 16
    assert D == KC * P and F == P and D == 2 * F and TOP * NT % 2 == 0 and E == B and E % 2 == 0 and TILES <= 2 * P and GU == 2 * D

    rows = nc.dram_tensor("expert_rows", (E * REGION + P, ROW), F32, kind="Internal").ap()
    results = nc.dram_tensor("expert_results", (TOP * T, D), F32, kind="Internal").ap()
    x_blocks = x.rearrange("b (j p) d -> p b j d", p=P)
    out_blocks = out.rearrange("b (j p) d -> p b j d", p=P)
    result_blocks = results.rearrange("(k b j p) d -> p k b j d", k=TOP, b=B, p=P)

    with ExitStack() as ctx:
        def sb(name, shape, dt=F32):
            return ctx.enter_context(nc.sbuf_tensor(name, shape, dt))

        def psum(name, shape, dt=F32):
            return ctx.enter_context(nc.psum_tensor(name, shape, dt))

        def sem(name):
            return ctx.enter_context(nc.semaphore(name))

        tokens = sb("tokens", [P, NT, D])
        w_hi = sb("w_hi", [P, E, GU], F32R)
        w_lo = sb("w_lo", [P, E, GU], F32R)
        w_down = sb("w_down", [P, E, D])
        all_logits = sb("all_logits", [P, NT, E])
        all_best = sb("all_best", [P, NT, TOP])
        prob = sb("prob", [P, TOP, NT])
        ident = sb("ident", [P, P])
        row_buf = sb("row_buf", [P, 2, J, ROW])
        fill_rows = sb("fill_rows", [P, ROW])
        fill_at = sb("fill_at", [1, E + 1], I32)
        ones_row = sb("ones_row", [P, E])
        tile_no_i = sb("tile_no_i", [P, 2], I32)
        tile_no = sb("tile_no", [P, 2])
        region_of_col = sb("region_of_col", [P, J, E])
        ones = sb("ones", [P, P], BF16)
        chosen_sum = sb("chosen_sum", [P, J, E], BF16)

        part_a = ctx.enter_context(ExitStack())

        def sb_a(name, shape, dt=F32):
            return part_a.enter_context(nc.sbuf_tensor(name, shape, dt))

        wab = sb_a("wab", [P, KC, 48])
        wgd = sb_a("wgd", [P, KC, 2 * D])
        wc = sb_a("wc", [N, D])
        wsh = sb_a("wsh", [P, KC, 2 * D])
        wshd = sb_a("wshd", [P, KC, D])
        wrt = sb_a("wrt", [P, KC, E])
        bias_parts = sb_a("bias_parts", [P, 2 * D], BF16)
        earlier = sb_a("earlier", [P, P], BF16)
        expert_of_col = sb_a("expert_of_col", [P, E])
        result_row = sb_a("result_row", [P, J], I32)
        raw_w = sb_a("raw_w", [P, 2, GU])
        xn = sb_a("xn", [P, J, D])
        xT = sb_a("xT", [P, KC, S])
        h2T = sb_a("h2T", [P, KC, S])
        states = sb_a("states", [N, S])
        moments = sb_a("moments", [P, 2, 2 * J, 2])
        raw1 = sb_a("raw1", [P, J, 6])
        raw2 = sb_a("raw2", [P, J, 6])
        rstd = sb_a("rstd", [P, 2 * J])
        half_var = sb_a("half_var", [P, 2 * J])
        newton_t = sb_a("newton_t", [P, 2 * J])
        gate_t = sb_a("gate_t", [P, 2, D])
        dx = sb_a("dx", [P, 2, D])
        xdx = sb_a("xdx", [P, 2, D])
        diff = sb_a("diff", [P, 2, D])
        act_s = sb_a("act_s", [P, 2, D])
        inner = sb_a("inner", [P, 2, D])
        innerT = sb_a("innerT", [P, 2, D])
        logits = sb_a("logits", [P, J, E])
        best = sb_a("best", [P, J, 8])
        best_at = sb_a("best_at", [P, J, 8], U32)
        chosen = sb_a("chosen", [P, TOP, J, E])
        chosen_any = sb_a("chosen_any", [P, J, E], BF16)
        place = sb_a("place", [P, J, E])
        placed = sb_a("placed", [P, TOP, J, E])
        slot = sb_a("slot", [P, 2, TOP, J], I32)
        part_a.close()

        bx = [sb(f"bx{a}", [P, 2, 2 * KC * P], F32R) for a in range(2)]
        b_silu = sb("b_silu", [P, 2, 2 * F])
        b_inner = sb("b_inner", [P, 2, 2 * F])
        b_innerT = sb("b_innerT", [P, 2, 2 * P])
        y = sb("y", [P, 4, 2, D])
        row_ids = sb("row_ids", [P, 8, 2], I32)
        res = sb("res", [P, 2, TOP, J, D])
        table = sb("table", [1, 4 * P], I32)
        per_expert = sb("per_expert", [P, 5, E])
        per_tile = sb("per_tile", [P, 2, 2, E])
        of_tile = sb("of_tile", [P, 4, 2])
        table_cols = sb("table_cols", [P, 4])

        tr = [psum(f"tr{i}", [P, 512]) for i in range(2)]
        gd = [psum(f"gd{i}", [P, 512]) for i in range(2)]
        cb = psum("cb", [P, 512])
        gu = psum("gu", [P, 512])
        dn = psum("dn", [P, 512])
        misc = psum("misc", [P, 512])

        x_in = [sem(f"x_in{i}") for i in range(2)]
        attn_w_in = sem("attn_w_in")
        ffn_w_in = sem("ffn_w_in")
        raw_w_in = [sem(f"raw_w_in{i}") for i in range(2)]
        const_step = sem("const_step")
        const_ready = sem("const_ready")
        bias_step = sem("bias_step")
        bias_ready = sem("bias_ready")
        w_down_in = sem("w_down_in")
        w_hi_ready = sem("w_hi_ready")
        w_lo_ready = sem("w_lo_ready")
        ln1_raw = sem("ln1_raw")
        ln1_moments = sem("ln1_moments")
        ln2_raw = sem("ln2_raw")
        ln2_moments = sem("ln2_moments")
        newton = sem("newton")
        xn_ready = sem("xn_ready")
        t1_done = sem("t1_done")
        xT_ready = sem("xT_ready")
        ab_done = sem("ab_done")
        decay_ready = sem("decay_ready")
        states_ready = sem("states_ready")
        gd_done = sem("gd_done")
        gate_ready = sem("gate_ready")
        dx_ready = sem("dx_ready")
        xdx_ready = sem("xdx_ready")
        c_done = sem("c_done")
        diff_ready = sem("diff_ready")
        gated_ready = sem("gated_ready")
        x1_ready = sem("x1_ready")
        h2_ready = sem("h2_ready")
        t2_done = sem("t2_done")
        h2T_ready = sem("h2T_ready")
        router_done = sem("router_done")
        logits_ready = sem("logits_ready")
        logits_kept = sem("logits_kept")
        best_ready = sem("best_ready")
        best_at_ready = sem("best_at_ready")
        chosen_ready = sem("chosen_ready")
        any_ready = sem("any_ready")
        rank_done = sem("rank_done")
        place_ready = sem("place_ready")
        sum_ready = sem("sum_ready")
        placed_ready = sem("placed_ready")
        slot_ready = sem("slot_ready")
        gu_done = sem("gu_done")
        silu_ready = sem("silu_ready")
        inner_ready = sem("inner_ready")
        th_done = sem("th_done")
        innerT_ready = sem("innerT_ready")
        dn_done = sem("dn_done")
        shared_added = sem("shared_added")
        dest_step = sem("dest_step")
        sent1 = [sem(f"sent1_{i}") for i in range(2)]
        sent2 = [sem(f"sent2_{i}") for i in range(2)]
        count_done = sem("count_done")
        tab_step = sem("tab_step")
        tab_cols = sem("tab_cols")
        tab_ready = sem("tab_ready")
        fill_ready = sem("fill_ready")
        filled = sem("filled")
        prob_step = sem("prob_step")
        prob_act = sem("prob_act")
        rows_in = [sem(f"rows_in{i}") for i in range(4)]
        bt_done = sem("bt_done")
        bx_hi = sem("bx_hi")
        bx_lo = sem("bx_lo")
        bgu_done = sem("bgu_done")
        bsilu = sem("bsilu")
        binner = sem("binner")
        bth_done = sem("bth_done")
        bh_ready = sem("bh_ready")
        bdn_done = sem("bdn_done")
        by_ready = sem("by_ready")
        ids_kept = sem("ids_kept")
        by_sent = [sem(f"by_sent{i}") for i in range(4)]
        res_in = [sem(f"res_in{i}") for i in range(2)]
        first_added = sem("first_added")
        both_added = sem("both_added")
        out_sent = sem("out_sent")

        NEWTON = 12
        block = ctx.enter_context(nc.Block())

        def wait_apart(eng, semaphore, value):
            eng.wait_ge(semaphore, value)
            eng.nop(nofuse=True)

        def known(s, least):
            return not isinstance(s, int) or s >= least

        def half_steps(eng, half):
            half(-1, 1)
            for s in range(3):
                half(s, s % 2, s // 2)
            with eng.Fori(1, (B - 4) // 2) as i:
                half(2 * i + 1, 1, i)
                half(2 * i + 2, 0, i + 1)
            for s in range(B - 3, B + 1):
                half(s, s % 2, s // 2)

        def has_front(s):
            return not isinstance(s, int) or s + 1 < B

        def has_back(s):
            return not isinstance(s, int) or 0 <= s < B

        def gu_bank(p):
            return gd[p][:].rearrange("q (h w) -> q h w", h=2)

        @block.sync
        def _(sp):
            def load_x(b, p, n):
                if known(b, 2):
                    wait_apart(sp, x_in[p], W * n)
                sp.dma_start(tokens[:, bass.ds(J * b, J), :], x_blocks[:, b, :, :]).then_inc(x_in[p], W)

            def load_expert(e, p, n):
                if known(e, 2):
                    wait_apart(sp, w_lo_ready, e - 1)
                gate_up = raw_w[:, p, :].rearrange("q (c g f) -> q c g f", c=KC, g=2)
                sp.dma_start(gate_up[:, :, 0, :], gate_w[e].rearrange("(c q) f -> q c f", q=P)).then_inc(raw_w_in[p], W)
                sp.dma_start(gate_up[:, :, 1, :], up_w[e].rearrange("(c q) f -> q c f", q=P)).then_inc(raw_w_in[p], W)
                sp.dma_start(w_down[:, bass.ds(e, 1), :], down_w[e][:, None, :]).then_inc(w_down_in, W)

            load_x(0, 0, 0)
            wait_apart(sp, const_ready, 1)
            sp.dma_start(wab[:, :, 0:N], wa_t.rearrange("(c q) n -> q c n", q=P)).then_inc(attn_w_in, W)
            sp.dma_start(wab[:, :, 32:32 + N], wb_t.rearrange("(c q) n -> q c n", q=P)).then_inc(attn_w_in, W)
            sp.dma_start(wgd[:], wgd_t.rearrange("(c q) n -> q c n", q=P)).then_inc(attn_w_in, W)
            for q in (0, 32, 64):
                sp.dma_start(xT[q:q + 1, 0, :], bias).then_inc(attn_w_in, W)
            sp.dma_start(wc[:], wc_t).then_inc(attn_w_in, W)
            load_x(1, 1, 0)
            sp.dma_start(wrt[:], router_w.rearrange("(c q) n -> q c n", q=P)).then_inc(ffn_w_in, W)
            sp.dma_start(wsh[:], shared_gu.rearrange("(c q) n -> q c n", q=P)).then_inc(ffn_w_in, W)
            sp.dma_start(wshd[:], shared_down.rearrange("(c q) n -> q c n", q=P)).then_inc(ffn_w_in, W)
            load_x(2, 0, 1)
            load_expert(0, 0, 0)
            load_expert(1, 1, 0)
            with sp.Fori(0, (B - 4) // 2) as i:
                load_x(2 * i + 3, 1, i + 1)
                load_x(2 * i + 4, 0, i + 2)
                load_expert(2 * i + 2, 0, i + 1)
                load_expert(2 * i + 3, 1, i + 1)
            load_x(B - 1, 1, B // 2 - 1)
            load_expert(B - 2, 0, B // 2 - 1)
            load_expert(B - 1, 1, B // 2 - 1)

            wait_apart(sp, fill_ready, 1)
            with sp.Fori(0, E + 1) as e:
                at = sp.value_load(fill_at[0:1, bass.ds(e, 1)], min_val=0, max_val=E * REGION)
                sp.dma_start(rows[bass.ds(at, P), :], fill_rows[:]).then_inc(filled, W)

            wait_apart(sp, filled, W * (E + 1))
            for p in range(2):
                wait_apart(sp, sent1[p], W * J * B // 2)
                wait_apart(sp, sent2[p], W * J * B // 2)
            wait_apart(sp, tab_ready, 1)
            regs = [sp.alloc_register(f"row_reg{k}") for k in range(4)]

            def load_two_pairs(i, m, n):
                sp.load(regs, table[0:1, bass.ds(4 * i, 4)])
                at = [sp.snap(r, min_val=0, max_val=E * REGION) for r in regs]
                for h in range(2):
                    w = 2 * m + h
                    if known(n, 1):
                        wait_apart(sp, bt_done, 2 * i + h - 3)
                        wait_apart(sp, ids_kept, 2 * i + h - 3)
                    for t in range(2):
                        b = 2 * h + t + 4 * m
                        sp.dma_start(row_buf[:, b // J, b % J, :], rows[bass.ds(at[2 * h + t], P), :]).then_inc(
                            rows_in[w], W)

            assert PAIRS % 4 == 0
            load_two_pairs(0, 0, 0)
            load_two_pairs(1, 1, 0)
            with sp.Fori(1, PAIRS // 4) as i:
                load_two_pairs(2 * i, 0, i)
                load_two_pairs(2 * i + 1, 1, i)

            for w in range(4):
                wait_apart(sp, by_sent[w], W * 2 * PAIRS // 4)
            wait_apart(sp, tab_ready, 1)

            def load_results(b, p, n):
                if known(n, 1):
                    wait_apart(sp, both_added, J * b - J)
                for k in range(TOP):
                    sp.dma_start(res[:, p, k], result_blocks[:, k, b, :, :]).then_inc(res_in[p], W)

            load_results(0, 0, 0)
            load_results(1, 1, 0)
            with sp.Fori(1, B // 2) as i:
                load_results(2 * i, 0, i)
                load_results(2 * i + 1, 1, i)
            wait_apart(sp, out_sent, W * B)

        @block.tensor
        def _(pe):
            def transposes(bank, at, src, sem_, n=1):
                for k, s in enumerate(src):
                    last = pe.transpose(bank[:, at + P * k:at + P * k + P], s, ident[:])
                last.then_inc(sem_, n)

            def shared_down_of(k, j):
                pe.wait_ge(innerT_ready, J * k + j + 1)
                if known(k, 1) or j:
                    pe.wait_ge(shared_added, J * k + j)
                for c in range(KC):
                    last = pe.matmul(dn[:, 0:D], innerT[:, j % 2, c * P:(c + 1) * P], wshd[:, c, :],
                                     start=c == 0, stop=c == KC - 1)
                last.then_inc(dn_done, 1)

            def half(s, p, n=0):
                f, k = s + 1, s
                front, back = has_front(s), has_back(s)
                last_back = isinstance(s, int) and s == B - 1

                def gate_and_dx(j):
                    if known(f, 1) or j >= 2:
                        pe.wait_ge(dx_ready, J * f + j - 1)
                    for c in range(KC):
                        pe.matmul(gd[j % 2][:], xT[:, c, j * P:(j + 1) * P], wgd[:, c, :], start=c == 0, stop=False)
                    pe.matmul(gd[j % 2][:], ones[:], bias_parts[:], start=False, stop=True).then_inc(gd_done, 1)

                def recurrent(j):
                    if known(f, 1) or j:
                        pe.wait_ge(diff_ready, J * f + j)
                    pe.matmul(cb[:, 0:D], states[:, j * P:(j + 1) * P], wc[:], start=True, stop=True).then_inc(c_done, 1)

                def shared_gate_up(j):
                    if known(k, 1) or j:
                        pe.wait_ge(inner_ready, J * k + j)
                    for c in range(KC):
                        last = pe.matmul(gu[:], h2T[:, c, j * P:(j + 1) * P], wsh[:, c, :],
                                         start=c == 0, stop=c == KC - 1)
                    last.then_inc(gu_done, 1)

                def inner_transposes(j):
                    pe.wait_ge(inner_ready, J * k + j + 1)
                    if j >= 2:
                        pe.wait_ge(innerT_ready, J * k + j - 1)
                    transposes(tr[j % 2], 0, [inner[:, j % 2, c * P:(c + 1) * P] for c in range(KC)], th_done)

                if front:
                    for g in range(2):
                        pe.wait_ge(xn_ready, J * f + 2 * g + 2)
                        if known(k, 1):
                            pe.wait_ge(innerT_ready, J * k - 1 + g)
                        elif known(k, 0):
                            pe.wait_ge(xT_ready, 2 * f - 1 + g)
                        transposes(tr[g], 0, [xn[:, 2 * g + h, c * P:(c + 1) * P]
                                              for h in range(2) for c in range(KC)], t1_done)
                if known(k, 1):
                    shared_down_of(k - 1, J - 1)
                if front:
                    pe.wait_ge(xT_ready, 2 * f + 2)
                    if known(k, 1):
                        pe.wait_ge(place_ready, k)
                    elif known(k, 0):
                        pe.wait_ge(states_ready, f)
                    for c in range(KC):
                        last = pe.matmul(misc[0:48, :], wab[:, c, :], xT[:, c, :], start=c == 0, stop=c == KC - 1)
                    last.then_inc(ab_done, 1)
                    gate_and_dx(0)
                    gate_and_dx(1)
                if back:
                    for g in range(2):
                        pe.wait_ge(h2_ready, J * k + 2 * g + 2)
                        if front:
                            pe.wait_ge(xT_ready, 2 * f + g + 1)
                        else:
                            pe.wait_ge(innerT_ready, J * k - 1 + g)
                        transposes(tr[g], 0, [row_buf[:, p, 2 * g + h, c * P:(c + 1) * P]
                                              for h in range(2) for c in range(KC)], t2_done)
                if front:
                    pe.wait_ge(states_ready, f + 1)
                    recurrent(0)
                if back:
                    pe.wait_ge(h2T_ready, 2 * k + 2)
                    if last_back:
                        pe.wait_ge(place_ready, k)
                    for j in range(J):
                        for c in range(KC):
                            last = pe.matmul(misc[:, j * E:(j + 1) * E], h2T[:, c, j * P:(j + 1) * P], wrt[:, c, :],
                                             start=c == 0, stop=c == KC - 1)
                    last.then_inc(router_done, 1)
                if front:
                    recurrent(1)
                if back:
                    shared_gate_up(0)
                if front:
                    gate_and_dx(2)
                    recurrent(2)
                if back:
                    shared_gate_up(1)
                    inner_transposes(0)
                if front:
                    gate_and_dx(3)
                    recurrent(3)
                if back:
                    pe.wait_ge(any_ready, k + 1)
                    ranks = misc[:, 0:J * E].rearrange("q (j e) -> q j e", e=E)
                    pe.matmul(ranks, earlier[:], chosen_any[:], start=True, stop=False)
                    for j in range(J - 1):
                        pe.matmul(ranks[:, j + 1:J, :], ones[:],
                                  chosen_any[:, j:j + 1, :].to_broadcast([P, J - 1 - j, E]), start=False, stop=False)
                    for j in range(J):
                        last = pe.matmul(ranks, ones[:], chosen_sum[:, j:j + 1, :].to_broadcast([P, J, E]),
                                         start=False, stop=j == J - 1)
                    last.then_inc(rank_done, 1)
                    shared_gate_up(2)
                    shared_down_of(k, 0)
                    inner_transposes(1)
                    shared_gate_up(3)
                    shared_down_of(k, 1)
                    inner_transposes(2)
                    shared_down_of(k, 2)
                    inner_transposes(3)

            pe.wait_ge(const_ready, 1)
            pe.wait_ge(attn_w_in, W * 7)
            pe.wait_ge(bias_ready, 3)
            pe.wait_ge(ffn_w_in, W * 3)
            half_steps(pe, half)

            pe.wait_ge(sum_ready, B)
            for j in range(J):
                last = pe.matmul(misc[:, 0:E], ones[:], chosen_sum[:, j, :], start=j == 0, stop=j == J - 1)
            last.then_inc(count_done, 1)
            pe.wait_ge(tab_cols, 1)
            for c in range(4):
                last = pe.matmul(misc[0:1, c * P:(c + 1) * P], table_cols[:, c:c + 1], ident[:],
                                 start=True, stop=True)
            last.then_inc(count_done, 1)

            PASSES = ((0, 0), (0, 1), (1, 0))
            gate_up_w = [w[:].rearrange("q e w -> q (e w)") for w in (w_hi, w_lo)]
            down_w_flat = w_down[:].rearrange("q e d -> q (e d)")
            btr, bgu, bth, bdn = (tr[0], tr[1]), (gd[0], gd[1]), cb, (gu, dn)
            regs = [pe.alloc_register(f"weight_reg{k}") for k in range(6)]

            def rows_transposed(q, w, p, n):
                pe.wait_ge(rows_in[w], 2 * W * (n + 1))
                if known(q, 2):
                    pe.wait_ge(bx_lo, q - 1)
                srcs = [row_buf[:, (2 * w + h) // J, (2 * w + h) % J, c * P:(c + 1) * P]
                        for h in range(2) for c in range(KC)]
                transposes(btr[p], 0, srcs, bt_done)

            def gate_up(q, p, at):
                pe.wait_ge(bx_lo, q + 1)
                if known(q, 2):
                    pe.wait_ge(binner, q - 1)
                for h in range(2):
                    steps = [(a, b, c) for a, b in PASSES for c in range(KC)]
                    for m, (a, b, c) in enumerate(steps):
                        last = pe.matmul(bgu[p][:, h * 2 * F:(h + 1) * 2 * F],
                                         bx[a][:, p, (h * KC + c) * P:(h * KC + c + 1) * P],
                                         gate_up_w[b][:, bass.ds(at[h] * 2 + c * 2 * F, 2 * F)],
                                         start=m == 0, stop=m == len(steps) - 1)
                last.then_inc(bgu_done, 1)

            def inner_turned(q, p):
                pe.wait_ge(binner, q + 1)
                if known(q, 1):
                    pe.wait_ge(bh_ready, q)
                transposes(bth, 0, [b_inner[:, p, h * F:(h + 1) * F] for h in range(2)], bth_done)

            def down(q, p, at):
                pe.wait_ge(bh_ready, q + 1)
                if known(q, 2):
                    pe.wait_ge(by_ready, q - 1)
                for h in range(2):
                    last = pe.matmul(bdn[p][:, h * D:(h + 1) * D], b_innerT[:, p, h * P:(h + 1) * P],
                                     down_w_flat[:, bass.ds(at[h], D)], start=True, stop=True)
                last.then_inc(bdn_done, 1)

            def weight_at(first, count):
                use = regs[:count]
                pe.load(use, table[0:1, bass.ds(first, count)])
                return [pe.snap(r, min_val=0, max_val=(E - 1) * D) for r in use]

            pe.wait_ge(tab_ready, 1)
            pe.wait_ge(w_lo_ready, E)
            pe.wait_ge(w_down_in, W * E)
            rows_transposed(0, 0, 0, 0)
            at = weight_at(2 * P, 4)
            rows_transposed(1, 1, 1, 0)
            gate_up(0, 0, at[0:2])
            rows_transposed(2, 2, 0, 0)
            inner_turned(0, 0)
            gate_up(1, 1, at[2:4])
            down(0, 0, at[0:2])

            def two_pairs(q, w, n, last=False):
                at = weight_at(2 * q + 2 * P - 2, 6)
                rows_transposed(q + 1, w + 1, 1, n)
                inner_turned(q - 1, 1)
                gate_up(q, 0, at[2:4])
                down(q - 1, 1, at[0:2])
                if not last:
                    rows_transposed(q + 2, (w + 2) % 4, 0, n + (w == 2))
                inner_turned(q, 0)
                gate_up(q + 1, 1, at[4:6])
                down(q, 0, at[2:4])

            two_pairs(2, 2, 0)
            with pe.Fori(1, PAIRS // 4 - 1) as i:
                two_pairs(4 * i, 0, i)
                two_pairs(4 * i + 2, 2, i)
            two_pairs(PAIRS - 4, 0, PAIRS // 4 - 1)
            two_pairs(PAIRS - 2, 2, PAIRS // 4 - 1, last=True)
            at = weight_at(2 * P + TILES - 2, 2)
            inner_turned(PAIRS - 1, 1)
            down(PAIRS - 1, 1, at)

        @block.scalar
        def _(act):
            def half(s, p, n=0):
                f, k = s + 1, s
                front, back = has_front(s), has_back(s)

                def gate_and_dx_out(j):
                    act.wait_ge(gd_done, J * f + j + 1)
                    if known(f, 1) or j >= 2:
                        act.wait_ge(gated_ready, J * f + j - 1)
                        act.wait_ge(xdx_ready, J * f + j - 1)
                    act.activation(gate_t[:, j % 2, :], gd[j % 2][:, 0:D], ACT.Tanh, scale=0.5).then_inc(gate_ready, 1)
                    act.activation(dx[:, j % 2, :], gd[j % 2][:, D:2 * D], ACT.Copy).then_inc(dx_ready, 1)

                def silu_out(j):
                    act.wait_ge(gu_done, J * k + j + 1)
                    if known(k, 1) or j >= 2:
                        act.wait_ge(inner_ready, J * k + j - 1)
                    act.activation(act_s[:, j % 2, :], gu[:, 0:D], ACT.Silu).then_inc(silu_ready, 1)

                def innerT_out(j):
                    act.wait_ge(th_done, J * k + j + 1)
                    if known(k, 1) or j >= 2:
                        act.wait_ge(dn_done, J * k + j - 1)
                    act.activation(innerT[:, j % 2, :], tr[j % 2][:, 0:D], ACT.Copy).then_inc(innerT_ready, 1)

                def turned_out(dst, bank, g, done):
                    act.activation(dst[:, :, g * 2 * P:(g + 1) * 2 * P].rearrange("q c (h t) -> q h c t", h=2),
                                   bank[:].rearrange("q (h c t) -> q h c t", h=2, c=KC), ACT.Copy).then_inc(done, 1)

                if front:
                    if known(f, 1):
                        act.wait_ge(gd_done, J * f)
                    for g in range(2):
                        act.wait_ge(t1_done, 2 * f + g + 1)
                        turned_out(xT, tr[g], g, xT_ready)
                    act.wait_ge(ab_done, f + 1)
                    if known(f, 1):
                        act.wait_ge(c_done, J * f)
                    act.activation(states[:], misc[0:N, :], ACT.Tanh).then_inc(decay_ready, 1)
                    gate_and_dx_out(0)
                    gate_and_dx_out(1)
                if back:
                    if known(k, 1):
                        act.wait_ge(gu_done, J * k)
                    for g in range(2):
                        act.wait_ge(t2_done, 2 * k + g + 1)
                        turned_out(h2T, tr[g], g, h2T_ready)
                    silu_out(0)
                if front:
                    gate_and_dx_out(2)
                if back:
                    act.wait_ge(raw_w_in[p], 2 * W * (n + 1))
                    act.activation(w_hi[:, k, :], raw_w[:, p, :], ACT.Copy).then_inc(w_hi_ready, 1)
                    silu_out(1)
                    innerT_out(0)
                if front:
                    gate_and_dx_out(3)
                if back:
                    silu_out(2)
                    innerT_out(1)
                    silu_out(3)
                    innerT_out(2)
                    innerT_out(3)

            half_steps(act, half)

            act.wait_ge(prob_step, 2)
            act.activation(all_logits[:], all_logits[:], ACT.Exp).then_inc(prob_act, 1)
            act.activation(prob[:, 1, :], prob[:, 1, :], ACT.Exp).then_inc(prob_act, 1)

            def pair(q, p, last=False, first=False):
                if not last:
                    act.wait_ge(bt_done, q + 2)
                    if known(q, 1):
                        act.wait_ge(bgu_done, q)
                    act.activation(bx[0][:, 1 - p, :], tr[1 - p][:], ACT.Copy).then_inc(bx_hi, 1)
                act.wait_ge(bgu_done, q + 1)
                if known(q, 2):
                    act.wait_ge(binner, q - 1)
                act.activation(b_silu[:, p, :].rearrange("q (h f) -> q h f", h=2),
                               gu_bank(p)[:, :, 0:F], ACT.Silu).then_inc(bsilu, 1)
                act.wait_ge(bth_done, q + 1)
                if known(q, 2):
                    act.wait_ge(bdn_done, q - 1)
                act.activation(b_innerT[:, p, :], cb[:, 0:2 * F], ACT.Copy).then_inc(bh_ready, 1)

            act.wait_ge(bt_done, 1)
            act.activation(bx[0][:, 0, :], tr[0][:], ACT.Copy).then_inc(bx_hi, 1)
            pair(0, 0)
            pair(1, 1)
            with act.Fori(1, PAIRS // 2 - 1) as i:
                pair(2 * i, 0)
                pair(2 * i + 1, 1)
            pair(PAIRS - 2, 0)
            pair(PAIRS - 1, 1, last=True)

            with act.Fori(0, B) as b:
                act.wait_ge(both_added, J * b + J)
                act.dma_start(out_blocks[:, b, :, :], tokens[:, bass.ds(J * b, J), :]).then_inc(out_sent, W)

        @block.vector
        def _(dve):
            dve.wait_ge(attn_w_in, W * 7)
            bias_f, rest = xT[:, 0, :], xT[:, 1, :]
            steps = 0

            def bias_link(ins):
                nonlocal steps
                steps += 1
                ins.then_inc(bias_step, 1)
                dve.wait_ge(bias_step, steps)

            part = h2T[:].rearrange("q c s -> q (c s)").bitcast(BF16)
            parts = [part[:, m * 2 * D:(m + 1) * 2 * D] for m in range(3)]
            bias_link(dve.tensor_copy(parts[0], bias_f))
            bias_link(dve.tensor_tensor(rest, bias_f, parts[0], ALU.subtract))
            bias_link(dve.tensor_copy(parts[1], rest))
            bias_link(dve.tensor_tensor(rest, rest, parts[1], ALU.subtract))
            bias_link(dve.tensor_copy(parts[2], rest))
            for m in range(3):
                dve.tensor_copy(bias_parts[32 * m:32 * m + 1, :], parts[m][32 * m:32 * m + 1, :]).then_inc(bias_ready, 1)

            def ln1_stats(b, p, n, j):
                if j == 0:
                    dve.wait_ge(x_in[p], W * (n + 1))
                if known(b, 1):
                    wait_apart(dve, ln1_moments, J * b - J + j + 1)
                dve.bn_stats(raw1[:, j, :], tokens[:, J * b + j, :]).then_inc(ln1_raw, 1)

            def ln1_means(b, p, j, m):
                wait_apart(dve, ln1_raw, J * b + j + 1)
                dve.bn_aggr(moments[:, m, J + j, :], raw1[:, j, :]).then_inc(ln1_moments, 1)

            def rsqrt_chain(h, p):
                at = NEWTON * h
                var = moments[:, p, :, 1]
                dve.tensor_scalar(half_var[:], var, -0.5, -0.5 * EPS, ALU.mult, ALU.add).then_inc(newton, 1)
                dve.tensor_scalar(newton_t[:], var, EPS, None, ALU.add).then_inc(newton, 1)
                dve.wait_ge(newton, at + 2)
                dve.tensor_scalar(rstd[:].bitcast(I32), newton_t[:].bitcast(I32), -0.5, RSQRT_SEED,
                                  ALU.mult, ALU.add).then_inc(newton, 1)
                for m in range(3):
                    dve.wait_ge(newton, at + 3 * m + 3)
                    dve.tensor_tensor(newton_t[:], rstd[:], rstd[:], ALU.mult).then_inc(newton, 1)
                    dve.wait_ge(newton, at + 3 * m + 4)
                    dve.tensor_tensor(newton_t[:], newton_t[:], half_var[:], ALU.mult).then_inc(newton, 1)
                    dve.wait_ge(newton, at + 3 * m + 5)
                    dve.scalar_tensor_tensor(rstd[:], newton_t[:], 1.5, rstd[:], ALU.add, ALU.mult).then_inc(newton, 1)

            def normalise(dst, b, p, j, col, done):
                dve.tensor_scalar(dst, tokens[:, J * b + j, :], moments[:, p, col, 0:1], rstd[:, col:col + 1],
                                  ALU.subtract, ALU.mult).then_inc(done, 1)

            def add_shared(k, j):
                dve.wait_ge(dn_done, J * k + j + 1)
                dve.tensor_tensor(tokens[:, J * k + j, :], tokens[:, J * k + j, :], dn[:, 0:D],
                                  ALU.add).then_inc(shared_added, 1)

            def half(s, p, n=0):
                f, k = s + 1, s
                front, back = has_front(s), has_back(s)
                stats_next = not isinstance(s, int) or s + 3 < B
                xn_next = not isinstance(s, int) or s + 2 < B
                n3 = (s + 3) // 2 if isinstance(s, int) else n + 1 + p

                def y_diff(j):
                    dve.wait_ge(c_done, J * f + j + 1)
                    dve.wait_ge(dx_ready, J * f + j + 1)
                    dve.tensor_tensor(diff[:, j % 2, :], cb[:, 0:D], dx[:, j % 2, :], ALU.subtract).then_inc(diff_ready, 1)

                def y_gated(j):
                    dve.wait_ge(gate_ready, J * f + j + 1)
                    dve.wait_ge(diff_ready, J * f + j + 1)
                    dve.scalar_tensor_tensor(diff[:, j % 2, :], gate_t[:, j % 2, :], 1.0, diff[:, j % 2, :],
                                             ALU.add, ALU.mult).then_inc(gated_ready, 1)

                def y_sum(j):
                    dve.wait_ge(gated_ready, J * f + j + 1)
                    dve.wait_ge(xdx_ready, J * f + j + 1)
                    dve.scalar_tensor_tensor(tokens[:, J * f + j, :], diff[:, j % 2, :], 0.5, xdx[:, j % 2, :],
                                             ALU.mult, ALU.add).then_inc(x1_ready, 1)

                def y_stats(j):
                    dve.wait_ge(x1_ready, J * f + j + 1)
                    if known(f, 1):
                        wait_apart(dve, ln2_moments, J * f - J + j + 1)
                    dve.bn_stats(raw2[:, j, :], tokens[:, J * f + j, :]).then_inc(ln2_raw, 1)

                def y_means(j):
                    wait_apart(dve, ln2_raw, J * f + j + 1)
                    dve.bn_aggr(moments[:, 1 - p, j, :], raw2[:, j, :]).then_inc(ln2_moments, 1)

                def gated_inner(j):
                    dve.wait_ge(silu_ready, J * k + j + 1)
                    if known(k, 1) or j >= 2:
                        dve.wait_ge(th_done, J * k + j - 1)
                    dve.tensor_tensor(inner[:, j % 2, :], gu[:, D:2 * D], act_s[:, j % 2, :],
                                      ALU.mult).then_inc(inner_ready, 1)

                def stats(j):
                    if stats_next:
                        ln1_stats(s + 3, 1 - p, n3, j)

                def means(j):
                    if stats_next:
                        ln1_means(s + 3, 1 - p, j, 1 - p)

                if back or xn_next:
                    if back:
                        dve.wait_ge(ln2_moments, J * k + J)
                    if xn_next:
                        dve.wait_ge(ln1_moments, J * (s + 2) + J)
                    rsqrt_chain(s + 2, p)
                    dve.wait_ge(newton, NEWTON * (s + 3))
                if back:
                    if known(k, 2):
                        dve.wait_ge(sent2[p], W * J * n)
                    for j in range(J):
                        normalise(row_buf[:, p, j, 0:D], k, p, j, j, h2_ready)
                if known(k, 1):
                    add_shared(k - 1, J - 1)
                if front:
                    dve.wait_ge(decay_ready, f + 1)
                    dve.tensor_tensor_scan(states[:], states[:], misc[32:32 + N, :], 0.0,
                                           ALU.mult, ALU.add).then_inc(states_ready, 1)
                    y_diff(0)
                    stats(0)
                    y_diff(1)
                    y_gated(0)
                    y_gated(1)
                    y_sum(0)
                    y_sum(1)
                    means(0)
                    y_stats(0)
                    y_stats(1)
                if back:
                    dve.wait_ge(router_done, k + 1)
                    if known(k, 1):
                        dve.wait_ge(logits_kept, 2 * k)
                    dve.tensor_copy(logits[:].rearrange("q j e -> q (j e)"), misc[:, 0:J * E]).then_inc(logits_ready, 1)
                if front:
                    y_means(0)
                    y_means(1)
                if back:
                    wait_apart(dve, logits_ready, k + 1)
                    for j in range(J):
                        dve.max(best[:, j, :], logits[:, j, :]).then_inc(best_ready, 1)
                    for j in range(J):
                        wait_apart(dve, best_ready, J * k + j + 1)
                        dve.max_index(best_at[:, j, :], best[:, j, :], logits[:, j, :]).then_inc(best_at_ready, 1)
                    gated_inner(0)
                    dve.wait_ge(best_at_ready, J * k + J)
                    dve.tensor_tensor(chosen[:], expert_of_col[:, None, None, :].to_broadcast([P, TOP, J, E]),
                                      best_at[:, :, 0:TOP].rearrange("q j k -> q k j")[:, :, :, None].to_broadcast(
                                          [P, TOP, J, E]), ALU.is_equal).then_inc(chosen_ready, 1)
                    stats(1)
                    dve.wait_ge(chosen_ready, k + 1)
                    dve.tensor_tensor(chosen_any[:], chosen[:, 0], chosen[:, 1], ALU.add).then_inc(any_ready, 1)
                else:
                    stats(1)
                if front:
                    y_diff(2)
                    means(1)
                    y_gated(2)
                if back:
                    gated_inner(1)
                if front:
                    y_sum(2)
                    stats(2)
                    y_stats(2)
                    y_diff(3)
                    y_means(2)
                    y_gated(3)
                    means(2)
                    y_sum(3)
                if back:
                    dve.wait_ge(rank_done, k + 1)
                    dve.tensor_tensor(place[:], misc[:, 0:J * E].rearrange("q (j e) -> q j e", e=E), region_of_col[:],
                                      ALU.add).then_inc(place_ready, 1)
                    dve.tensor_tensor(chosen_sum[:], chosen_sum[:], chosen_any[:], ALU.add).then_inc(sum_ready, 1)
                    dve.wait_ge(place_ready, k + 1)
                    dve.tensor_tensor(placed[:], chosen[:], place[:, None, :, :].to_broadcast([P, TOP, J, E]),
                                      ALU.mult).then_inc(placed_ready, 1)
                if front:
                    y_stats(3)
                if back:
                    dve.wait_ge(placed_ready, k + 1)
                    with nc.allow_low_precision(reason="one integer below 2 ** 24 and zeros"):
                        dve.tensor_reduce(slot[:, p], placed[:], AX_X, ALU.add).then_inc(slot_ready, 1)
                if front:
                    y_means(3)
                if back:
                    gated_inner(2)
                    add_shared(k, 0)
                stats(3)
                if back:
                    gated_inner(3)
                    add_shared(k, 1)
                means(3)
                if xn_next:
                    dve.wait_ge(t1_done, 2 * f + 2)
                    for j in range(J):
                        normalise(xn[:, j, :], s + 2, p, j, J + j, xn_ready)
                if back:
                    add_shared(k, 2)

            dve.wait_ge(const_ready, 1)
            for b in range(2):
                for j in range(J):
                    ln1_stats(b, b, 0, j)
                for j in range(J):
                    ln1_means(b, b, j, b)
            dve.wait_ge(ln1_moments, J)
            rsqrt_chain(0, 0)
            dve.wait_ge(newton, NEWTON)
            for j in range(J):
                normalise(xn[:, j, :], 0, 0, j, J + j, xn_ready)
            half_steps(dve, half)

            step = 0

            def link(ins):
                nonlocal step
                step += 1
                ins.then_inc(tab_step, 1)
                dve.wait_ge(tab_step, step)

            cnt, ntile, upto, stride = (per_expert[:, m, :] for m in range(4))
            up = per_expert[:, 4, :].bitcast(I32)
            before, weighted = per_tile[:, 0], per_tile[:, 1]
            expert, row0, first = (of_tile[:, m, :] for m in range(3))
            dve.wait_ge(count_done, 1)
            link(dve.tensor_copy(cnt, misc[:, 0:E]))
            dve.tensor_tensor(fill_at[0:1, 0:E], cnt[0:1], region_of_col[0:1, 0, :], ALU.add).then_inc(fill_ready, 1)
            link(dve.tensor_scalar(up, cnt, float(P - 1), None, ALU.add))
            link(dve.tensor_scalar(up, up, 7, None, ALU.logical_shift_right))
            link(dve.tensor_copy(ntile, up))
            link(dve.tensor_scalar(stride, ntile, -float(P), float(REGION), ALU.mult, ALU.add))
            link(dve.tensor_tensor_scan(upto, ones_row[:], ntile, 0.0, ALU.mult, ALU.add))
            link(dve.tensor_tensor(before, upto[:, None, :].to_broadcast([P, 2, E]),
                                   tile_no[:, :, None].to_broadcast([P, 2, E]), ALU.is_le))
            link(dve.tensor_tensor(weighted, before, stride[:, None, :].to_broadcast([P, 2, E]), ALU.mult))
            link(dve.tensor_reduce(expert, before, AX_X, ALU.add))
            link(dve.tensor_reduce(row0, weighted, AX_X, ALU.add))
            link(dve.scalar_tensor_tensor(first, tile_no[:], float(P), row0, ALU.mult, ALU.add))
            link(dve.tensor_scalar(table_cols[:, 0:2], first, float(E * REGION), None, ALU.min))
            dve.tensor_scalar(table_cols[:, 2:4], expert, float(E - 1), float(D), ALU.min, ALU.mult).then_inc(tab_cols, 1)
            dve.wait_ge(count_done, 2)
            dve.tensor_copy(table[:], misc[0:1, :]).then_inc(tab_ready, 1)

            dve.wait_ge(logits_kept, 2 * B)
            dve.tensor_tensor(all_logits[:], all_logits[:], all_best[:, :, 0:1].to_broadcast([P, NT, E]),
                              ALU.subtract).then_inc(prob_step, 1)
            dve.tensor_tensor(prob[:, 1, :], all_best[:, :, 1], all_best[:, :, 0], ALU.subtract).then_inc(prob_step, 1)

            def rows_rest(p):
                dve.tensor_tensor(bx[1][:, p, :], tr[p][:], bx[0][:, p, :].bitcast(F32), ALU.subtract).then_inc(bx_lo, 1)

            def results_out(q, w, n):
                p = w % 2
                dve.wait_ge(bdn_done, q + 1)
                if known(n, 1):
                    dve.wait_ge(by_sent[w], 2 * W * n)
                dve.tensor_copy(y[:, w], (gu, dn)[p][:].rearrange("q (h d) -> q h d", h=2)).then_inc(by_ready, 1)

            def pair(q, w, n, last=False):
                p = w % 2
                if not last:
                    dve.wait_ge(bx_hi, q + 2)
                    rows_rest(1 - p)
                if known(q, 1):
                    results_out(q - 1, (w + 3) % 4, n if w else n - 1)
                dve.wait_ge(bsilu, q + 1)
                if known(q, 2):
                    dve.wait_ge(bth_done, q - 1)
                dve.tensor_tensor(b_inner[:, p, :].rearrange("q (h f) -> q h f", h=2), gu_bank(p)[:, :, F:2 * F],
                                  b_silu[:, p, :].rearrange("q (h f) -> q h f", h=2), ALU.mult).then_inc(binner, 1)

            dve.wait_ge(bx_hi, 1)
            rows_rest(0)
            pair(0, 0, 0)
            dve.wait_ge(prob_act, 2)
            dve.tensor_reduce(prob[:, 0, :], all_logits[:], AX_X, ALU.add).then_inc(prob_step, 1)
            dve.wait_ge(prob_step, 3)
            dve.reciprocal(prob[:, 0, :], prob[:, 0, :]).then_inc(prob_step, 1)
            dve.wait_ge(prob_step, 4)
            dve.tensor_tensor(prob[:, 1, :], prob[:, 1, :], prob[:, 0, :], ALU.mult).then_inc(prob_step, 1)
            pair(1, 1, 0)
            for q in range(2, 8):
                pair(q, q % 4, q // 4)
            with dve.Fori(2, PAIRS // 4 - 1) as i:
                for w in range(4):
                    pair(4 * i + w, w, i)
            for q in range(PAIRS - 4, PAIRS):
                pair(q, q % 4, q // 4, last=q == PAIRS - 1)
            results_out(PAIRS - 1, 3, PAIRS // 4 - 1)

            def combine(b, p, n):
                dve.wait_ge(res_in[p], TOP * W * (n + 1))
                for k, done in enumerate((first_added, both_added)):
                    for j in range(J):
                        if k:
                            dve.wait_ge(first_added, J * b + j + 1)
                        tok = tokens[:, J * b + j, :]
                        dve.scalar_tensor_tensor(tok, res[:, p, k, j, :], prob[:, k, bass.ds(J * b + j, 1)], tok,
                                                 ALU.mult, ALU.add).then_inc(done, 1)

            dve.wait_ge(prob_step, 5)
            with dve.Fori(0, B // 2) as i:
                combine(2 * i, 0, i)
                combine(2 * i + 1, 1, i)

        @block.gpsimd
        def _(pool):
            steps = 0

            def link(ins):
                nonlocal steps
                steps += 1
                ins.then_inc(const_step, 1)
                wait_apart(pool, const_step, steps)

            link(pool.memset(ident[:], 0.0))
            link(pool.affine_select(out=ident[:], in_=ident[:], compare_op=ALU.not_equal, fill=1.0, base=0,
                                    pattern=[[-1, P]], channel_multiplier=1))
            link(pool.memset(ones[:], 1.0))
            link(pool.affine_select(out=earlier[:], in_=ones[:], compare_op=ALU.is_gt, fill=0.0, base=0,
                                    pattern=[[1, P]], channel_multiplier=-1))
            link(pool.memset(chosen_sum[:], 0.0))
            link(pool.memset(bias_parts[:], 0.0))
            link(pool.memset(xT[:], 0.0))
            link(pool.memset(fill_rows[:, 0:D], 0.0))
            link(pool.memset(fill_rows[:, D:ROW].bitcast(I32), NOWHERE))
            link(pool.memset(ones_row[:], 1.0))
            link(pool.iota(tile_no_i[:], pattern=[[P, 2]], base=0, channel_multiplier=1))
            link(pool.tensor_copy(tile_no[:], tile_no_i[:]))
            link(pool.memset(wab[:], 0.0))
            link(pool.memset(moments[:], 1.0))
            link(pool.memset(row_buf[:, :, :, D:ROW], 0.0))
            link(pool.memset(fill_at[:], E * REGION))
            it = slot[:].rearrange("q a k j -> q (a k j)")
            assert E <= 2 * TOP * J
            link(pool.iota(it[:, 0:E], pattern=[[1, E]], base=0, channel_multiplier=0))
            link(pool.tensor_copy(expert_of_col[:], it[:, 0:E]))
            for j in range(J):
                link(pool.tensor_scalar(region_of_col[:, j, :], expert_of_col[:], float(REGION), None, ALU.mult))
            pool.iota(result_row[:], pattern=[[P, J]], base=0, channel_multiplier=1).then_inc(const_ready, 1)

            def half(s, p, n=0):
                f, k = s + 1, s
                front, back = has_front(s), has_back(s)

                def x_plus_dx(j):
                    wait_apart(pool, dx_ready, J * f + j + 1)
                    if known(f, 1) or j >= 2:
                        wait_apart(pool, x1_ready, J * f + j - 1)
                    pool.tensor_tensor(xdx[:, j % 2, :], tokens[:, J * f + j, :], dx[:, j % 2, :],
                                       ALU.add).then_inc(xdx_ready, 1)

                def send(choice, j, done):
                    pool.indirect_dma_start(
                        out=rows, out_offset=bass.IndirectOffsetOnAxis(ap=slot[:, p, choice, j:j + 1], axis=0),
                        in_=row_buf[:, p, j, :], in_offset=None).then_inc(done, W)

                if back:
                    if known(k, 2):
                        wait_apart(pool, sent2[p], W * J * n)
                    pool.tensor_copy(row_buf[:, p, :, D].bitcast(I32), result_row[:]).then_inc(dest_step, 1)
                    wait_apart(pool, dest_step, 3 * k + 1)
                    pool.tensor_scalar(result_row[:], result_row[:], S, None, ALU.add).then_inc(dest_step, 1)
                if front:
                    x_plus_dx(0)
                    x_plus_dx(1)
                if back:
                    wait_apart(pool, logits_ready, k + 1)
                    pool.tensor_copy(all_logits[:, bass.ds(J * k, J), :], logits[:]).then_inc(logits_kept, 1)
                    wait_apart(pool, best_at_ready, J * k + J)
                    pool.tensor_copy(all_best[:, bass.ds(J * k, J), :], best[:, :, 0:TOP]).then_inc(logits_kept, 1)
                if front:
                    x_plus_dx(2)
                if back:
                    wait_apart(pool, w_hi_ready, k + 1)
                    pool.tensor_tensor(w_lo[:, k, :], raw_w[:, p, :], w_hi[:, k, :].bitcast(F32),
                                       ALU.subtract).then_inc(w_lo_ready, 1)
                if front:
                    x_plus_dx(3)
                if back:
                    wait_apart(pool, slot_ready, k + 1)
                    wait_apart(pool, h2_ready, J * k + J)
                    wait_apart(pool, dest_step, 3 * k + 2)
                    for j in range(J):
                        send(0, j, sent1[p])
                    wait_apart(pool, sent1[p], W * J * (n + 1))
                    wait_apart(pool, t2_done, 2 * k + 2)
                    pool.tensor_scalar(row_buf[:, p, :, D].bitcast(I32), row_buf[:, p, :, D].bitcast(I32), T, None,
                                       ALU.add).then_inc(dest_step, 1)
                    wait_apart(pool, dest_step, 3 * k + 3)
                    for j in range(J):
                        send(1, j, sent2[p])

            half_steps(pool, half)

            def keep_ids(q, w, n, at):
                wait_apart(pool, rows_in[w], 2 * W * (n + 1))
                if known(q, 8):
                    wait_apart(pool, by_sent[w], 2 * W * (n - 1))
                pool.tensor_copy(row_ids[:, at, :], row_buf[:, w // 2, 2 * (w % 2):2 * (w % 2) + 2, D].bitcast(I32)).then_inc(
                    ids_kept, 1)

            def send_pair(q, w, at):
                wait_apart(pool, by_ready, q + 1)
                wait_apart(pool, ids_kept, q + 1)
                for h in range(2):
                    pool.indirect_dma_start(
                        out=results, out_offset=bass.IndirectOffsetOnAxis(ap=row_ids[:, at, h:h + 1], axis=0),
                        in_=y[:, w, h, :], in_offset=None, bounds_check=TOP * T - 1,
                        oob_is_err=False).then_inc(by_sent[w], W)

            AHEAD = 4
            assert PAIRS % 8 == 0
            for q in range(AHEAD):
                keep_ids(q, q, 0, q)
            for q in range(8):
                keep_ids(q + AHEAD, q % 4, q // 4 + 1, (q + AHEAD) % 8)
                send_pair(q, q % 4, q)
            with pool.Fori(1, PAIRS // 8 - 1) as i:
                for m in range(8):
                    keep_ids(8 * i + m + AHEAD, m % 4, 2 * i + m // 4 + 1, (m + AHEAD) % 8)
                    send_pair(8 * i + m, m % 4, m)
            for q in range(PAIRS - 8, PAIRS):
                if q + AHEAD < PAIRS:
                    keep_ids(q + AHEAD, q % 4, q // 4 + 1, (q + AHEAD) % 8)
                send_pair(q, q % 4, q % 8)


def kernel(**inputs):
    import numpy as _np
    import concourse.bacc as _bacc
    from concourse import mybir as _mybir
    from concourse.bass_utils import run_bass_kernel_spmd as _run

    a = {k: _np.asarray(v) for k, v in inputs.items()}
    laid = {
        "x": a["L0_attn_x"],
        "wa_t": a["L0_attn_WA"].T,
        "wb_t": a["L0_attn_WB"].T,
        "wc_t": a["L0_attn_WC"].T,
        "wgd_t": _np.concatenate([a["L0_attn_Wg"].T, a["L0_attn_WD"].T], axis=1),
        "bias": _np.concatenate([a["L0_attn_bg"], a["L0_attn_bD"]])[None],
        "router_w": a["L0_ffn_router_w"],
        "gate_w": a["L0_ffn_gate_w"],
        "up_w": a["L0_ffn_up_w"],
        "down_w": a["L0_ffn_down_w"],
        "shared_gu": _np.concatenate([a["L0_ffn_shared_gate_w"], a["L0_ffn_shared_up_w"]], axis=1),
        "shared_down": a["L0_ffn_shared_down_w"],
    }
    nc = _bacc.Bacc("TRN2", target_bir_lowering=False, num_devices=1)
    arrays, args = {}, []
    for name, v in laid.items():
        v = _np.ascontiguousarray(v)
        arrays[f"in_{name}"] = v
        args.append(nc.dram_tensor(f"in_{name}", v.shape, _mybir.dt.from_np(v.dtype), kind="ExternalInput").ap())
    args.append(nc.dram_tensor("out_0", laid["x"].shape, _mybir.dt.float32, kind="ExternalOutput").ap())
    preln_gated_scan_and_routed_experts(nc, *args)
    r = _run(nc, [arrays], core_ids=[0])
    return r.results[0]["out_0"]
```

```python
from contextlib import ExitStack

import concourse.bass as bass
from concourse import mybir

ALU = mybir.AluOpType
ACT = mybir.ActivationFunctionType
AX_X = mybir.AxisListType.X
F32 = mybir.dt.float32
F32R = mybir.dt.float32r
BF16 = mybir.dt.bfloat16
I32 = mybir.dt.int32
U32 = mybir.dt.uint32

P = 128
EPS = 1e-5
RSQRT_SEED = 1597463007.0


def preln_gated_scan_and_routed_experts(nc, x, wa_t, wb_t, wc_t, wgd_t, bias, router_w, gate_w, up_w, down_w,
                                        shared_gu, shared_down, out):
    B, S, D = x.shape
    N = wa_t.shape[1]
    E = router_w.shape[1]
    F = gate_w.shape[2]
    TOP = 2
    T = B * S
    KC = D // P
    J = S // P
    NT = T // P
    TILES = TOP * NT + E
    PAIRS = TILES // 2
    REGION = T + P
    ROW = D + 4
    GU = KC * 2 * F
    NOWHERE = 2 ** 30
    W = 16
    assert D == KC * P and F == P and D == 2 * F and TOP * NT % 2 == 0 and E == B and E % 2 == 0 and TILES <= 2 * P and GU == 2 * D

    rows = nc.dram_tensor("expert_rows", (E * REGION + P, ROW), F32, kind="Internal").ap()
    results = nc.dram_tensor("expert_results", (TOP * T, D), F32, kind="Internal").ap()
    x_blocks = x.rearrange("b (j p) d -> p b j d", p=P)
    out_blocks = out.rearrange("b (j p) d -> p b j d", p=P)
    result_blocks = results.rearrange("(k b j p) d -> p k b j d", k=TOP, b=B, p=P)

    with ExitStack() as ctx:
        def sb(name, shape, dt=F32):
            return ctx.enter_context(nc.sbuf_tensor(name, shape, dt))

        def psum(name, shape, dt=F32):
            return ctx.enter_context(nc.psum_tensor(name, shape, dt))

        def sem(name):
            return ctx.enter_context(nc.semaphore(name))

        tokens = sb("tokens", [P, NT, D])
        raw_w = sb("raw_w", [P, E, GU])
        w_down = sb("w_down", [P, E, D])
        all_logits = sb("all_logits", [P, NT, E])
        all_best = sb("all_best", [P, NT, TOP])
        prob = sb("prob", [P, TOP, NT])
        ident = sb("ident", [P, P])
        row_buf = sb("row_buf", [P, 2, J, ROW])
        fill_rows = sb("fill_rows", [P, ROW])
        fill_at = sb("fill_at", [1, E + 1], I32)
        ones_row = sb("ones_row", [P, E])
        tile_no_i = sb("tile_no_i", [P, 2], I32)
        tile_no = sb("tile_no", [P, 2])
        region_of_col = sb("region_of_col", [P, J, E])
        ones = sb("ones", [P, P], BF16)
        chosen_sum = sb("chosen_sum", [P, J, E], BF16)
        slot = sb("slot", [P, 2, TOP, J], I32)
        result_row = sb("result_row", [P, J], I32)

        part_a = ctx.enter_context(ExitStack())

        def sb_a(name, shape, dt=F32):
            return part_a.enter_context(nc.sbuf_tensor(name, shape, dt))

        wgd = [sb_a(f"wgd{a}", [P, KC, 2 * D], F32R) for a in range(2)]
        xT = [sb_a(f"xT{a}", [P, KC, S], F32R) for a in range(2)]
        xn = sb_a("xn", [P, J, D])
        wab = [sb_a(f"wab{a}", [P, KC, P], F32R) for a in range(2)]
        state_parts = sb_a("state_parts", [P, S], F32R)
        states = sb_a("states", [N, S])
        wc_parts = sb_a("wc_parts", [P, D], F32R)
        dx = sb_a("dx", [P, 2, D])
        xdx = sb_a("xdx", [P, 2, D])
        gate_t = sb_a("gate_t", [P, 2, D])
        diff = sb_a("diff", [P, 2, D])
        bias_parts = sb_a("bias_parts", [P, 2 * D], BF16)
        wsh = [sb_a(f"wsh{a}", [P, KC, 2 * D], F32R) for a in range(2)]
        h2T = [sb_a(f"h2T{a}", [P, KC, S], F32R) for a in range(2)]
        wshd = [sb_a(f"wshd{a}", [P, KC, D], F32R) for a in range(2)]
        innerT = [sb_a(f"innerT{a}", [P, 2, D], F32R) for a in range(2)]
        act_s = sb_a("act_s", [P, 2, D])
        inner = sb_a("inner", [P, 2, D])
        wrt = [sb_a(f"wrt{a}", [P, KC, E], F32R) for a in range(2)]
        moments = sb_a("moments", [P, 2, 2 * J, 2])
        raw1 = sb_a("raw1", [P, J, 6])
        raw2 = sb_a("raw2", [P, J, 6])
        rstd = sb_a("rstd", [P, 2 * J])
        shift = sb_a("shift", [P, 2 * J])
        half_var = sb_a("half_var", [P, 2 * J])
        newton_t = sb_a("newton_t", [P, 2 * J])
        earlier = sb_a("earlier", [P, P], BF16)
        expert_of_col = sb_a("expert_of_col", [P, E])
        logits = sb_a("logits", [P, J, E])
        best = sb_a("best", [P, J, 8])
        best_at = sb_a("best_at", [P, J, 8], U32)
        chosen = sb_a("chosen", [P, TOP, J, E])
        chosen_any = sb_a("chosen_any", [P, J, E], BF16)
        place = sb_a("place", [P, J, E])
        placed = sb_a("placed", [P, TOP, J, E])
        part_a.close()

        def staged(b, size, at=0):
            return tokens[:, J * b:J * b + J, :].rearrange("q j d -> q (j d)")[:, at:at + size]

        bias_f, bias_rest = staged(B - 1, 2 * D), staged(B - 1, 2 * D, 2 * D)
        bias_thirds = staged(B - 2, 3 * D).bitcast(BF16)
        raw_wgd, raw_wsh = staged(B - 3, 4 * D), staged(B - 4, 4 * D)
        raw_wshd, raw_wab, raw_wc = staged(B - 5, 2 * D), staged(B - 5, KC * P, 2 * D), staged(B - 5, D, 3 * D)
        raw_wrt, zeros = staged(B - 6, KC * E), staged(B - 6, S, S)
        wc_hi = h2T[0][:, 0, 0:D]

        w_hi = sb("w_hi", [P, E, GU], F32R)
        w_lo = sb("w_lo", [P, E, GU], F32R)
        bx = [sb(f"bx{a}", [P, 2, 2 * KC * P], F32R) for a in range(2)]
        b_innerT = sb("b_innerT", [P, 2, 2 * P])
        row_ids = sb("row_ids", [P, 8, 2], I32)
        late = raw_w[:].rearrange("q e w -> q (e w)")
        res = late[:, 0:2 * TOP * J * D].rearrange("q (p k j d) -> q p k j d", p=2, k=TOP, j=J)
        late = late[:, 2 * TOP * J * D:E * GU]
        y = late[:, 0:8 * D].rearrange("q (w h d) -> q w h d", w=4, h=2)
        b_silu = late[:, 8 * D:8 * D + 4 * F].rearrange("q (p w) -> q p w", p=2)
        b_inner = late[:, 8 * D + 4 * F:8 * D + 8 * F].rearrange("q (p w) -> q p w", p=2)
        table = sb("table", [1, 4 * P], I32)
        per_expert = sb("per_expert", [P, 5, E])
        per_tile = sb("per_tile", [P, 2, 2, E])
        of_tile = sb("of_tile", [P, 4, 2])
        table_cols = sb("table_cols", [P, 4])

        tr = [psum(f"tr{i}", [P, 512]) for i in range(2)]
        gd = [psum(f"gd{i}", [P, 512]) for i in range(2)]
        cb = psum("cb", [P, 512])
        gu = psum("gu", [P, 512])
        dn = psum("dn", [P, 512])
        misc = psum("misc", [P, 512])

        x_in = [sem(f"x_in{i}") for i in range(2)]
        attn_w_in = sem("attn_w_in")
        ffn_w_in = sem("ffn_w_in")
        raw_w_in = sem("raw_w_in")
        stage_zeroed = sem("stage_zeroed")
        hi_split = sem("hi_split")
        lo_split = sem("lo_split")
        const_step = sem("const_step")
        const_ready = sem("const_ready")
        bias_step = sem("bias_step")
        bias_ready = sem("bias_ready")
        w_down_in = sem("w_down_in")
        w_hi_ready = sem("w_hi_ready")
        w_lo_ready = sem("w_lo_ready")
        ln1_raw = sem("ln1_raw")
        ln1_moments = sem("ln1_moments")
        ln2_raw = sem("ln2_raw")
        ln2_moments = sem("ln2_moments")
        newton = sem("newton")
        xn_ready = sem("xn_ready")
        t1_done = sem("t1_done")
        xT_hi = sem("xT_hi")
        xT_ready = sem("xT_ready")
        ab_done = sem("ab_done")
        decay_ready = sem("decay_ready")
        scanned = sem("scanned")
        states_hi = sem("states_hi")
        states_ready = sem("states_ready")
        gd_done = sem("gd_done")
        gate_ready = sem("gate_ready")
        dx_ready = sem("dx_ready")
        xdx_ready = sem("xdx_ready")
        c_done = sem("c_done")
        diff_ready = sem("diff_ready")
        gated_ready = sem("gated_ready")
        x1_ready = sem("x1_ready")
        h2_ready = sem("h2_ready")
        t2_done = sem("t2_done")
        h2T_hi = sem("h2T_hi")
        h2T_ready = sem("h2T_ready")
        router_done = sem("router_done")
        logits_ready = sem("logits_ready")
        logits_kept = sem("logits_kept")
        best_ready = sem("best_ready")
        best_at_ready = sem("best_at_ready")
        chosen_ready = sem("chosen_ready")
        any_ready = sem("any_ready")
        rank_done = sem("rank_done")
        place_ready = sem("place_ready")
        sum_ready = sem("sum_ready")
        placed_ready = sem("placed_ready")
        slot_ready = sem("slot_ready")
        gu_done = sem("gu_done")
        silu_ready = sem("silu_ready")
        inner_ready = sem("inner_ready")
        th_done = sem("th_done")
        innerT_hi = sem("innerT_hi")
        innerT_ready = sem("innerT_ready")
        dn_done = sem("dn_done")
        shared_added = sem("shared_added")
        first_id = sem("first_id")
        result_row_ready = sem("result_row_ready")
        second_id = sem("second_id")
        sent1 = [sem(f"sent1_{i}") for i in range(2)]
        sent2 = [sem(f"sent2_{i}") for i in range(2)]
        count_done = sem("count_done")
        tab_step = sem("tab_step")
        tab_cols = sem("tab_cols")
        tab_ready = sem("tab_ready")
        fill_ready = sem("fill_ready")
        filled = sem("filled")
        prob_step = sem("prob_step")
        prob_act = sem("prob_act")
        rows_in = [sem(f"rows_in{i}") for i in range(4)]
        bt_done = sem("bt_done")
        bx_hi = sem("bx_hi")
        bx_lo = sem("bx_lo")
        bgu_done = sem("bgu_done")
        bsilu = sem("bsilu")
        binner = sem("binner")
        bth_done = sem("bth_done")
        bh_ready = sem("bh_ready")
        bdn_done = sem("bdn_done")
        by_ready = sem("by_ready")
        ids_kept = sem("ids_kept")
        by_sent = [sem(f"by_sent{i}") for i in range(4)]
        res_in = [sem(f"res_in{i}") for i in range(2)]
        first_added = sem("first_added")
        both_added = sem("both_added")
        out_sent = sem("out_sent")

        NEWTON = 13
        SPLITS = 6
        PASSES = ((0, 0), (0, 1), (1, 0))
        shared_bank = (gu, tr[1])
        block = ctx.enter_context(nc.Block())

        def wait_apart(eng, semaphore, value):
            eng.wait_ge(semaphore, value)
            eng.nop(nofuse=True)

        def known(s, least):
            return not isinstance(s, int) or s >= least

        def half_steps(eng, half):
            half(-1, 1)
            for s in range(3):
                half(s, s % 2, s // 2)
            with eng.Fori(1, (B - 4) // 2) as i:
                half(2 * i + 1, 1, i)
                half(2 * i + 2, 0, i + 1)
            for s in range(B - 3, B + 1):
                half(s, s % 2, s // 2)

        def has_front(s):
            return not isinstance(s, int) or s + 1 < B

        def has_back(s):
            return not isinstance(s, int) or 0 <= s < B

        def gu_bank(p):
            return gd[p][:].rearrange("q (h w) -> q h w", h=2)

        @block.sync
        def _(sp):
            def load_x(b, p, n):
                if known(b, 2):
                    wait_apart(sp, x_in[p], W * n)
                sp.dma_start(tokens[:, bass.ds(J * b, J), :], x_blocks[:, b, :, :]).then_inc(x_in[p], W)

            def load_expert(e):
                gate_up = raw_w[:, bass.ds(e, 1), :].rearrange("q e (c g f) -> q e c g f", c=KC, g=2)[:, 0]
                sp.dma_start(gate_up[:, :, 0, :], gate_w[e].rearrange("(c q) f -> q c f", q=P)).then_inc(raw_w_in, W)
                sp.dma_start(gate_up[:, :, 1, :], up_w[e].rearrange("(c q) f -> q c f", q=P)).then_inc(raw_w_in, W)
                sp.dma_start(w_down[:, bass.ds(e, 1), :], down_w[e][:, None, :]).then_inc(w_down_in, W)

            load_x(0, 0, 0)
            sp.dma_start(raw_wgd.rearrange("q (c n) -> q c n", c=KC), wgd_t.rearrange("(c q) n -> q c n", q=P)).then_inc(
                attn_w_in, W)
            wait_apart(sp, stage_zeroed, 3)
            for q in (0, 32, 64):
                sp.dma_start(bias_f[q:q + 1, :], bias).then_inc(attn_w_in, W)
                sp.dma_start(raw_wc[q:q + N, :], wc_t).then_inc(attn_w_in, W)
            ab = raw_wab.rearrange("q (c n) -> q c n", c=KC)
            sp.dma_start(ab[:, :, 0:N], wa_t.rearrange("(c q) n -> q c n", q=P)).then_inc(attn_w_in, W)
            sp.dma_start(ab[:, :, 32:32 + N], wb_t.rearrange("(c q) n -> q c n", q=P)).then_inc(attn_w_in, W)
            load_x(1, 1, 0)
            sp.dma_start(raw_wrt.rearrange("q (c n) -> q c n", c=KC), router_w.rearrange("(c q) n -> q c n", q=P)).then_inc(
                ffn_w_in, W)
            sp.dma_start(raw_wsh.rearrange("q (c n) -> q c n", c=KC), shared_gu.rearrange("(c q) n -> q c n", q=P)).then_inc(
                ffn_w_in, W)
            sp.dma_start(raw_wshd.rearrange("q (c n) -> q c n", c=KC), shared_down.rearrange("(c q) n -> q c n", q=P)).then_inc(
                ffn_w_in, W)
            load_x(2, 0, 1)
            wait_apart(sp, lo_split, SPLITS)
            with sp.Fori(0, (B - 4) // 2) as i:
                load_x(2 * i + 3, 1, i + 1)
                load_x(2 * i + 4, 0, i + 2)
                load_expert(2 * i)
                load_expert(2 * i + 1)
            load_x(B - 1, 1, B // 2 - 1)
            for e in range(B - 4, B):
                load_expert(e)

            wait_apart(sp, fill_ready, 1)
            with sp.Fori(0, E + 1) as e:
                at = sp.value_load(fill_at[0:1, bass.ds(e, 1)], min_val=0, max_val=E * REGION)
                sp.dma_start(rows[bass.ds(at, P), :], fill_rows[:]).then_inc(filled, W)

            wait_apart(sp, filled, W * (E + 1))
            for p in range(2):
                wait_apart(sp, sent1[p], W * J * B // 2)
                wait_apart(sp, sent2[p], W * J * B // 2)
            wait_apart(sp, tab_ready, 1)
            regs = [sp.alloc_register(f"row_reg{k}") for k in range(4)]

            def load_two_pairs(i, m, n):
                sp.load(regs, table[0:1, bass.ds(4 * i, 4)])
                at = [sp.snap(r, min_val=0, max_val=E * REGION) for r in regs]
                for h in range(2):
                    w = 2 * m + h
                    if known(n, 1):
                        wait_apart(sp, bt_done, 2 * i + h - 3)
                        wait_apart(sp, ids_kept, 2 * i + h - 3)
                    for t in range(2):
                        b = 2 * h + t + 4 * m
                        sp.dma_start(row_buf[:, b // J, b % J, :], rows[bass.ds(at[2 * h + t], P), :]).then_inc(
                            rows_in[w], W)

            assert PAIRS % 4 == 0
            load_two_pairs(0, 0, 0)
            load_two_pairs(1, 1, 0)
            with sp.Fori(1, PAIRS // 4) as i:
                load_two_pairs(2 * i, 0, i)
                load_two_pairs(2 * i + 1, 1, i)

            for w in range(4):
                wait_apart(sp, by_sent[w], W * 2 * PAIRS // 4)
            wait_apart(sp, tab_ready, 1)

            def load_results(b, p, n):
                if known(n, 1):
                    wait_apart(sp, both_added, J * b - J)
                for k in range(TOP):
                    sp.dma_start(res[:, p, k], result_blocks[:, k, b, :, :]).then_inc(res_in[p], W)

            load_results(0, 0, 0)
            load_results(1, 1, 0)
            with sp.Fori(1, B // 2) as i:
                load_results(2 * i, 0, i)
                load_results(2 * i + 1, 1, i)
            wait_apart(sp, out_sent, W * B)

        @block.tensor
        def _(pe):
            def transposes(bank, at, src, sem_, n=1):
                for k, s in enumerate(src):
                    last = pe.transpose(bank[:, at + P * k:at + P * k + P], s, ident[:])
                last.then_inc(sem_, n)

            def three_passes(dst, lhs, rhs):
                steps = [(a, b, c) for a, b in PASSES for c in range(KC)]
                for m, (a, b, c) in enumerate(steps):
                    last = pe.matmul(dst, lhs(a, c), rhs(b, c), start=m == 0, stop=m == len(steps) - 1)
                return last

            def shared_down_of(k, j):
                pe.wait_ge(innerT_ready, J * k + j + 1)
                if known(k, 1) or j:
                    pe.wait_ge(shared_added, J * k + j)
                three_passes(dn[:, 0:D], lambda a, c: innerT[a][:, j % 2, c * P:(c + 1) * P],
                             lambda b, c: wshd[b][:, c, :]).then_inc(dn_done, 1)

            def inner_transposes(k, j):
                pe.wait_ge(inner_ready, J * k + j + 1)
                if j:
                    pe.wait_ge(innerT_ready, J * k + j)
                transposes(cb, 0, [inner[:, j % 2, c * P:(c + 1) * P] for c in range(KC)], th_done)

            def half(s, p, n=0):
                f, k = s + 1, s
                front, back, tail = has_front(s), has_back(s), known(s, 1)
                last_back = isinstance(s, int) and s == B - 1

                def gate_and_dx(j):
                    if known(f, 1) or j >= 2:
                        pe.wait_ge(dx_ready, J * f + j - 1)
                    for a, b in PASSES:
                        for c in range(KC):
                            pe.matmul(gd[j % 2][:], xT[a][:, c, j * P:(j + 1) * P], wgd[b][:, c, :],
                                      start=(a, b, c) == (0, 0, 0), stop=False)
                    pe.matmul(gd[j % 2][:], ones[:], bias_parts[:], start=False, stop=True).then_inc(gd_done, 1)

                def recurrent(j):
                    if known(f, 1) or j:
                        pe.wait_ge(diff_ready, J * f + j)
                    pe.matmul(cb[:, 0:D], state_parts[0:96, j * P:(j + 1) * P], wc_parts[0:96, :],
                              start=True, stop=True).then_inc(c_done, 1)

                def shared_gate_up(j):
                    if known(k, 1) or j >= 2:
                        pe.wait_ge(inner_ready, J * k + j - 1)
                    three_passes(shared_bank[j % 2][:], lambda a, c: h2T[a][:, c, j * P:(j + 1) * P],
                                 lambda b, c: wsh[b][:, c, :]).then_inc(gu_done, 1)

                def front_transposes(g):
                    pe.wait_ge(xn_ready, J * f + 2 * g + 2)
                    if tail:
                        if g == 0:
                            pe.wait_ge(h2T_ready, 2 * k - 1)
                        else:
                            pe.wait_ge(inner_ready, J * k)
                    elif known(k, 0):
                        pe.wait_ge(xT_ready, 2 * f - 1 + g)
                    transposes(tr[g], 0, [xn[:, 2 * g + h, c * P:(c + 1) * P]
                                          for h in range(2) for c in range(KC)], t1_done)

                if front:
                    front_transposes(0)
                if tail:
                    inner_transposes(k - 1, 2)
                if front:
                    front_transposes(1)
                if tail:
                    shared_down_of(k - 1, 1)
                    inner_transposes(k - 1, 3)
                if front:
                    pe.wait_ge(xT_ready, 2 * f + 2)
                    if tail:
                        pe.wait_ge(place_ready, k)
                    elif known(k, 0):
                        pe.wait_ge(scanned, f)
                    three_passes(misc[:], lambda a, c: wab[a][:, c, :], lambda b, c: xT[b][:, c, :]).then_inc(ab_done, 1)
                if tail:
                    shared_down_of(k - 1, 2)
                def back_transposes(g):
                    pe.wait_ge(h2_ready, J * k + 2 * g + 2)
                    if front:
                        pe.wait_ge(xT_ready, 2 * f + g + 1)
                    elif g == 0:
                        pe.wait_ge(h2T_ready, 2 * k - 1)
                    else:
                        pe.wait_ge(inner_ready, J * k)
                    transposes(tr[g], 0, [row_buf[:, p, 2 * g + h, c * P:(c + 1) * P]
                                          for h in range(2) for c in range(KC)], t2_done)

                if front:
                    gate_and_dx(0)
                if back:
                    back_transposes(0)
                if tail:
                    shared_down_of(k - 1, 3)
                if back:
                    back_transposes(1)
                if front:
                    gate_and_dx(1)
                    pe.wait_ge(states_ready, f + 1)
                    pe.wait_ge(states_hi, 2 * f + 2)
                    if tail:
                        pe.wait_ge(innerT_ready, J * k)
                    recurrent(0)
                    gate_and_dx(2)
                    recurrent(1)
                if back:
                    pe.wait_ge(h2T_ready, 2 * k + 2)
                    if last_back:
                        pe.wait_ge(place_ready, k)
                    for j in range(J):
                        last = three_passes(misc[:, j * E:(j + 1) * E], lambda a, c: h2T[a][:, c, j * P:(j + 1) * P],
                                            lambda b, c: wrt[b][:, c, :])
                    last.then_inc(router_done, 1)
                    shared_gate_up(0)
                if front:
                    recurrent(2)
                    gate_and_dx(3)
                if back:
                    shared_gate_up(1)
                if front:
                    recurrent(3)
                if back:
                    pe.wait_ge(any_ready, k + 1)
                    ranks = misc[:, 0:J * E].rearrange("q (j e) -> q j e", e=E)
                    pe.matmul(ranks, earlier[:], chosen_any[:], start=True, stop=False)
                    for j in range(J - 1):
                        pe.matmul(ranks[:, j + 1:J, :], ones[:],
                                  chosen_any[:, j:j + 1, :].to_broadcast([P, J - 1 - j, E]), start=False, stop=False)
                    for j in range(J):
                        last = pe.matmul(ranks, ones[:], chosen_sum[:, j:j + 1, :].to_broadcast([P, J, E]),
                                         start=False, stop=j == J - 1)
                    last.then_inc(rank_done, 1)
                    shared_gate_up(2)
                    if front:
                        pe.wait_ge(diff_ready, J * f + J)
                    else:
                        pe.wait_ge(innerT_ready, J * k)
                    inner_transposes(k, 0)
                    shared_gate_up(3)
                    inner_transposes(k, 1)
                    shared_down_of(k, 0)

            pe.wait_ge(const_ready, 1)
            pe.wait_ge(bias_ready, 3)
            pe.wait_ge(lo_split, SPLITS)
            half_steps(pe, half)

            pe.wait_ge(sum_ready, B)
            for j in range(J):
                last = pe.matmul(misc[:, 0:E], ones[:], chosen_sum[:, j, :], start=j == 0, stop=j == J - 1)
            last.then_inc(count_done, 1)
            pe.wait_ge(tab_cols, 1)
            for c in range(4):
                last = pe.matmul(misc[0:1, c * P:(c + 1) * P], table_cols[:, c:c + 1], ident[:],
                                 start=True, stop=True)
            last.then_inc(count_done, 1)

            gate_up_w = [w[:].rearrange("q e w -> q (e w)") for w in (w_hi, w_lo)]
            down_w_flat = w_down[:].rearrange("q e d -> q (e d)")
            btr, bgu, bth, bdn = (tr[0], tr[1]), (gd[0], gd[1]), cb, (gu, dn)
            regs = [pe.alloc_register(f"weight_reg{k}") for k in range(6)]

            def rows_transposed(q, w, p, n):
                pe.wait_ge(rows_in[w], 2 * W * (n + 1))
                if known(q, 2):
                    pe.wait_ge(bx_lo, q - 1)
                srcs = [row_buf[:, (2 * w + h) // J, (2 * w + h) % J, c * P:(c + 1) * P]
                        for h in range(2) for c in range(KC)]
                transposes(btr[p], 0, srcs, bt_done)

            def gate_up(q, p, at):
                pe.wait_ge(bx_lo, q + 1)
                if known(q, 2):
                    pe.wait_ge(binner, q - 1)
                for h in range(2):
                    steps = [(a, b, c) for a, b in PASSES for c in range(KC)]
                    for m, (a, b, c) in enumerate(steps):
                        last = pe.matmul(bgu[p][:, h * 2 * F:(h + 1) * 2 * F],
                                         bx[a][:, p, (h * KC + c) * P:(h * KC + c + 1) * P],
                                         gate_up_w[b][:, bass.ds(at[h] * 2 + c * 2 * F, 2 * F)],
                                         start=m == 0, stop=m == len(steps) - 1)
                last.then_inc(bgu_done, 1)

            def inner_turned(q, p):
                pe.wait_ge(binner, q + 1)
                if known(q, 1):
                    pe.wait_ge(bh_ready, q)
                transposes(bth, 0, [b_inner[:, p, h * F:(h + 1) * F] for h in range(2)], bth_done)

            def down(q, p, at):
                pe.wait_ge(bh_ready, q + 1)
                if known(q, 2):
                    pe.wait_ge(by_ready, q - 1)
                for h in range(2):
                    last = pe.matmul(bdn[p][:, h * D:(h + 1) * D], b_innerT[:, p, h * P:(h + 1) * P],
                                     down_w_flat[:, bass.ds(at[h], D)], start=True, stop=True)
                last.then_inc(bdn_done, 1)

            def weight_at(first, count):
                use = regs[:count]
                pe.load(use, table[0:1, bass.ds(first, count)])
                return [pe.snap(r, min_val=0, max_val=(E - 1) * D) for r in use]

            pe.wait_ge(tab_ready, 1)
            pe.wait_ge(w_lo_ready, E // 2)
            pe.wait_ge(w_down_in, W * E)
            rows_transposed(0, 0, 0, 0)
            at = weight_at(2 * P, 4)
            rows_transposed(1, 1, 1, 0)
            gate_up(0, 0, at[0:2])
            rows_transposed(2, 2, 0, 0)
            inner_turned(0, 0)
            gate_up(1, 1, at[2:4])
            down(0, 0, at[0:2])

            def two_pairs(q, w, n, last=False):
                at = weight_at(2 * q + 2 * P - 2, 6)
                rows_transposed(q + 1, w + 1, 1, n)
                inner_turned(q - 1, 1)
                gate_up(q, 0, at[2:4])
                down(q - 1, 1, at[0:2])
                if not last:
                    rows_transposed(q + 2, (w + 2) % 4, 0, n + (w == 2))
                inner_turned(q, 0)
                gate_up(q + 1, 1, at[4:6])
                down(q, 0, at[2:4])

            two_pairs(2, 2, 0)
            with pe.Fori(1, PAIRS // 4 - 1) as i:
                two_pairs(4 * i, 0, i)
                two_pairs(4 * i + 2, 2, i)
            two_pairs(PAIRS - 4, 0, PAIRS // 4 - 1)
            two_pairs(PAIRS - 2, 2, PAIRS // 4 - 1, last=True)
            at = weight_at(2 * P + TILES - 2, 2)
            inner_turned(PAIRS - 1, 1)
            down(PAIRS - 1, 1, at)

        @block.scalar
        def _(act):
            def normalise(dst, b, j, col, done):
                act.activation(dst, tokens[:, J * b + j, :], ACT.Identity, scale=rstd[:, col:col + 1],
                               bias=shift[:, col:col + 1]).then_inc(done, 1)

            def innerT_out(k, j):
                act.wait_ge(th_done, J * k + j + 1)
                if known(k, 1) or j >= 2:
                    act.wait_ge(dn_done, J * k + j - 1)
                act.activation(innerT[0][:, j % 2, :], cb[:, 0:D], ACT.Copy).then_inc(innerT_hi, 1)

            def half(s, p, n=0):
                f, k = s + 1, s
                front, back, tail = has_front(s), has_back(s), known(s, 1)
                last_back = isinstance(s, int) and s == B - 1
                xn_next = not isinstance(s, int) or s + 2 < B

                def gate_and_dx_out(j):
                    act.wait_ge(gd_done, J * f + j + 1)
                    if known(f, 1) or j >= 2:
                        act.wait_ge(gated_ready, J * f + j - 1)
                        act.wait_ge(xdx_ready, J * f + j - 1)
                    act.activation(gate_t[:, j % 2, :], gd[j % 2][:, 0:D], ACT.Tanh, scale=0.5).then_inc(gate_ready, 1)
                    act.activation(dx[:, j % 2, :], gd[j % 2][:, D:2 * D], ACT.Copy).then_inc(dx_ready, 1)

                def silu_out(j):
                    act.wait_ge(gu_done, J * k + j + 1)
                    if known(k, 1) or j >= 2:
                        act.wait_ge(inner_ready, J * k + j - 1)
                    act.activation(act_s[:, j % 2, :], shared_bank[j % 2][:, 0:D], ACT.Silu).then_inc(silu_ready, 1)

                def turned_out(dst, bank, g, done):
                    act.activation(dst[:, :, g * 2 * P:(g + 1) * 2 * P].rearrange("q c (h t) -> q h c t", h=2),
                                   bank[:].rearrange("q (h c t) -> q h c t", h=2, c=KC), ACT.Copy).then_inc(done, 1)

                if front:
                    if known(f, 1):
                        act.wait_ge(gd_done, J * f)
                    act.wait_ge(t1_done, 2 * f + 1)
                    turned_out(xT[0], tr[0], 0, xT_hi)
                if tail:
                    innerT_out(k - 1, 2)
                if front:
                    act.wait_ge(t1_done, 2 * f + 2)
                    turned_out(xT[0], tr[1], 1, xT_hi)
                if tail:
                    innerT_out(k - 1, 3)
                if back:
                    act.wait_ge(newton, NEWTON * (s + 3))
                    if known(k, 2):
                        act.wait_ge(sent2[p], W * J * n)
                    for j in range(J):
                        normalise(row_buf[:, p, j, 0:D], k, j, j, h2_ready)
                if front:
                    act.wait_ge(ab_done, f + 1)
                    if known(f, 1):
                        act.wait_ge(states_ready, f)
                        act.wait_ge(states_hi, 2 * f)
                    act.activation(states[:], misc[0:N, :], ACT.Tanh).then_inc(decay_ready, 1)
                    act.wait_ge(scanned, f + 1)
                    if known(f, 1):
                        act.wait_ge(c_done, J * f)
                    for q in (0, 64):
                        act.activation(state_parts[q:q + N, :], states[:], ACT.Copy).then_inc(states_hi, 1)
                    gate_and_dx_out(0)
                if back:
                    if known(k, 1):
                        act.wait_ge(gu_done, J * k)
                    for g in range(2):
                        act.wait_ge(t2_done, 2 * k + g + 1)
                        turned_out(h2T[0], tr[g], g, h2T_hi)
                if front:
                    gate_and_dx_out(1)
                    gate_and_dx_out(2)
                if xn_next:
                    act.wait_ge(newton, NEWTON * (s + 3))
                    act.wait_ge(t1_done, 2 * f + 2)
                    for j in range(J):
                        normalise(xn[:, j, :], s + 2, j, J + j, xn_ready)
                if back:
                    silu_out(0)
                if front:
                    gate_and_dx_out(3)
                if back:
                    silu_out(1)
                    silu_out(2)
                    innerT_out(k, 0)
                    silu_out(3)
                    innerT_out(k, 1)
                if last_back:
                    act.wait_ge(raw_w_in, 2 * W * E)
                    act.wait_ge(c_done, J * B)
                    act.wait_ge(ln2_moments, J * B)
                    for e in range(0, E, 2):
                        act.activation(w_hi[:, e:e + 2, :], raw_w[:, e:e + 2, :], ACT.Copy).then_inc(w_hi_ready, 1)

            act.wait_ge(attn_w_in, W * 9)
            act.wait_ge(stage_zeroed, 4)
            act.activation(wab[0][:], raw_wab.rearrange("q (c n) -> q c n", c=KC), ACT.Copy).then_inc(hi_split, 1)
            act.activation(wgd[0][:], raw_wgd.rearrange("q (c n) -> q c n", c=KC), ACT.Copy).then_inc(hi_split, 1)
            act.activation(wc_hi, raw_wc, ACT.Copy).then_inc(hi_split, 1)
            act.activation(wc_parts[0:64, :], raw_wc[0:64, :], ACT.Copy).then_inc(hi_split, 1)
            act.activation(state_parts[:], zeros, ACT.Copy).then_inc(hi_split, 1)
            act.wait_ge(hi_split, 5)
            act.wait_ge(ffn_w_in, W * 3)
            act.activation(wrt[0][:], raw_wrt.rearrange("q (c n) -> q c n", c=KC), ACT.Copy).then_inc(hi_split, 1)
            act.activation(wsh[0][:], raw_wsh.rearrange("q (c n) -> q c n", c=KC), ACT.Copy).then_inc(hi_split, 1)
            act.activation(wshd[0][:], raw_wshd.rearrange("q (c n) -> q c n", c=KC), ACT.Copy).then_inc(hi_split, 1)
            act.wait_ge(newton, NEWTON)
            act.wait_ge(x_in[0], W)
            for j in range(J):
                normalise(xn[:, j, :], 0, j, J + j, xn_ready)
            half_steps(act, half)

            act.wait_ge(prob_step, 2)
            act.activation(all_logits[:], all_logits[:], ACT.Exp).then_inc(prob_act, 1)
            act.activation(prob[:, 1, :], prob[:, 1, :], ACT.Exp).then_inc(prob_act, 1)

            def pair(q, p, last=False, first=False):
                if not last:
                    act.wait_ge(bt_done, q + 2)
                    if known(q, 1):
                        act.wait_ge(bgu_done, q)
                    act.activation(bx[0][:, 1 - p, :], tr[1 - p][:], ACT.Copy).then_inc(bx_hi, 1)
                act.wait_ge(bgu_done, q + 1)
                if known(q, 2):
                    act.wait_ge(binner, q - 1)
                act.activation(b_silu[:, p, :].rearrange("q (h f) -> q h f", h=2),
                               gu_bank(p)[:, :, 0:F], ACT.Silu).then_inc(bsilu, 1)
                act.wait_ge(bth_done, q + 1)
                if known(q, 2):
                    act.wait_ge(bdn_done, q - 1)
                act.activation(b_innerT[:, p, :], cb[:, 0:2 * F], ACT.Copy).then_inc(bh_ready, 1)

            act.wait_ge(bt_done, 1)
            act.activation(bx[0][:, 0, :], tr[0][:], ACT.Copy).then_inc(bx_hi, 1)
            pair(0, 0)
            pair(1, 1)
            with act.Fori(1, PAIRS // 2 - 1) as i:
                pair(2 * i, 0)
                pair(2 * i + 1, 1)
            pair(PAIRS - 2, 0)
            pair(PAIRS - 1, 1, last=True)

            with act.Fori(0, B) as b:
                act.wait_ge(both_added, J * b + J)
                act.dma_start(out_blocks[:, b, :, :], tokens[:, bass.ds(J * b, J), :]).then_inc(out_sent, W)

        @block.vector
        def _(dve):
            dve.memset(raw_wab, 0.0).then_inc(stage_zeroed, 1)
            dve.memset(staged(B - 5, D, 3 * D), 0.0).then_inc(stage_zeroed, 1)
            dve.memset(staged(B - 1, 4 * D), 0.0).then_inc(stage_zeroed, 1)
            dve.memset(zeros, 0.0).then_inc(stage_zeroed, 1)

            def ln1_stats(b, p, n, j):
                if j == 0:
                    dve.wait_ge(x_in[p], W * (n + 1))
                if known(b, 1):
                    wait_apart(dve, ln1_moments, J * b - J + j + 1)
                dve.bn_stats(raw1[:, j, :], tokens[:, J * b + j, :]).then_inc(ln1_raw, 1)

            def ln1_means(b, p, j, m):
                wait_apart(dve, ln1_raw, J * b + j + 1)
                dve.bn_aggr(moments[:, m, J + j, :], raw1[:, j, :]).then_inc(ln1_moments, 1)

            def newton_op(h, p, m):
                mean, var = moments[:, p, :, 0], moments[:, p, :, 1]
                if m >= 2:
                    dve.wait_ge(newton, NEWTON * h + m)
                if m == 0:
                    ins = dve.tensor_scalar(half_var[:], var, -0.5, -0.5 * EPS, ALU.mult, ALU.add)
                elif m == 1:
                    ins = dve.tensor_scalar(newton_t[:], var, EPS, None, ALU.add)
                elif m == 2:
                    ins = dve.tensor_scalar(rstd[:].bitcast(I32), newton_t[:].bitcast(I32), -0.5, RSQRT_SEED,
                                            ALU.mult, ALU.add)
                elif m == NEWTON - 1:
                    ins = dve.scalar_tensor_tensor(shift[:], mean, -1.0, rstd[:], ALU.mult, ALU.mult)
                elif m % 3 == 0:
                    ins = dve.tensor_tensor(newton_t[:], rstd[:], rstd[:], ALU.mult)
                elif m % 3 == 1:
                    ins = dve.tensor_tensor(newton_t[:], newton_t[:], half_var[:], ALU.mult)
                else:
                    ins = dve.scalar_tensor_tensor(rstd[:], newton_t[:], 1.5, rstd[:], ALU.add, ALU.mult)
                ins.then_inc(newton, 1)

            def innerT_rest(k, j):
                dve.wait_ge(innerT_hi, J * k + j + 1)
                dve.tensor_tensor(innerT[1][:, j % 2, :], cb[:, 0:D], innerT[0][:, j % 2, :].bitcast(F32),
                                  ALU.subtract).then_inc(innerT_ready, 1)

            def turned_rest(dst, bank, g):
                at = slice(g * 2 * P, (g + 1) * 2 * P)
                return dve.tensor_tensor(dst[1][:, :, at].rearrange("q c (h t) -> q h c t", h=2),
                                         bank[:].rearrange("q (h c t) -> q h c t", h=2, c=KC),
                                         dst[0][:, :, at].rearrange("q c (h t) -> q h c t", h=2).bitcast(F32), ALU.subtract)

            def add_shared(k, j):
                dve.wait_ge(dn_done, J * k + j + 1)
                dve.tensor_tensor(tokens[:, J * k + j, :], tokens[:, J * k + j, :], dn[:, 0:D],
                                  ALU.add).then_inc(shared_added, 1)

            def half(s, p, n=0):
                f, k = s + 1, s
                front, back, tail = has_front(s), has_back(s), known(s, 1)
                stats_next = not isinstance(s, int) or s + 3 < B
                xn_next = not isinstance(s, int) or s + 2 < B
                n3 = (s + 3) // 2 if isinstance(s, int) else n + 1 + p

                def y_diff(j):
                    dve.wait_ge(c_done, J * f + j + 1)
                    dve.wait_ge(dx_ready, J * f + j + 1)
                    dve.tensor_tensor(diff[:, j % 2, :], cb[:, 0:D], dx[:, j % 2, :], ALU.subtract).then_inc(diff_ready, 1)

                def y_gated(j):
                    dve.wait_ge(gate_ready, J * f + j + 1)
                    dve.wait_ge(diff_ready, J * f + j + 1)
                    dve.scalar_tensor_tensor(diff[:, j % 2, :], gate_t[:, j % 2, :], 1.0, diff[:, j % 2, :],
                                             ALU.add, ALU.mult).then_inc(gated_ready, 1)

                def y_sum(j):
                    dve.wait_ge(gated_ready, J * f + j + 1)
                    dve.wait_ge(xdx_ready, J * f + j + 1)
                    dve.scalar_tensor_tensor(tokens[:, J * f + j, :], diff[:, j % 2, :], 0.5, xdx[:, j % 2, :],
                                             ALU.mult, ALU.add).then_inc(x1_ready, 1)

                def y_stats(j):
                    dve.wait_ge(x1_ready, J * f + j + 1)
                    if known(f, 1):
                        wait_apart(dve, ln2_moments, J * f - J + j + 1)
                    dve.bn_stats(raw2[:, j, :], tokens[:, J * f + j, :]).then_inc(ln2_raw, 1)

                def y_means(j):
                    wait_apart(dve, ln2_raw, J * f + j + 1)
                    dve.bn_aggr(moments[:, 1 - p, j, :], raw2[:, j, :]).then_inc(ln2_moments, 1)

                def gated_inner(j):
                    dve.wait_ge(silu_ready, J * k + j + 1)
                    if known(k, 1) or j >= 2:
                        dve.wait_ge(th_done, J * k + j - 1)
                    dve.tensor_tensor(inner[:, j % 2, :], shared_bank[j % 2][:, D:2 * D], act_s[:, j % 2, :],
                                      ALU.mult).then_inc(inner_ready, 1)

                def stats(j):
                    if stats_next:
                        ln1_stats(s + 3, 1 - p, n3, j)

                def means(j):
                    if stats_next:
                        ln1_means(s + 3, 1 - p, j, 1 - p)

                if front:
                    dve.wait_ge(xT_hi, 2 * f + 1)
                    turned_rest(xT, tr[0], 0).then_inc(xT_ready, 1)
                if back:
                    newton_op(s + 2, p, 10)
                if tail:
                    innerT_rest(k - 1, 2)
                if back:
                    newton_op(s + 2, p, 11)
                if front:
                    dve.wait_ge(xT_hi, 2 * f + 2)
                    turned_rest(xT, tr[1], 1).then_inc(xT_ready, 1)
                if back:
                    newton_op(s + 2, p, 12)
                if tail:
                    add_shared(k - 1, 1)
                    innerT_rest(k - 1, 3)
                stats(0)
                if tail:
                    add_shared(k - 1, 2)
                if front:
                    dve.wait_ge(decay_ready, f + 1)
                    dve.tensor_tensor_scan(states[:], states[:], misc[32:32 + N, :], 0.0,
                                           ALU.mult, ALU.add).then_inc(scanned, 1)
                stats(1)
                means(0)
                if front:
                    dve.wait_ge(states_hi, 2 * f + 1)
                    dve.tensor_tensor(state_parts[32:32 + N, :], states[:], state_parts[0:N, :].bitcast(F32),
                                      ALU.subtract).then_inc(states_ready, 1)
                means(1)
                if back:
                    dve.wait_ge(h2T_hi, 2 * k + 1)
                    turned_rest(h2T, tr[0], 0).then_inc(h2T_ready, 1)
                if tail:
                    add_shared(k - 1, 3)
                if back:
                    dve.wait_ge(h2T_hi, 2 * k + 2)
                    turned_rest(h2T, tr[1], 1).then_inc(h2T_ready, 1)
                stats(2)
                if front:
                    y_diff(0)
                    y_gated(0)
                    y_sum(0)
                    y_diff(1)
                    y_stats(0)
                    y_gated(1)
                    y_means(0)
                    stats(3)
                    y_sum(1)
                    means(2)
                    means(3)
                    y_stats(1)
                if back:
                    dve.wait_ge(router_done, k + 1)
                    if known(k, 1):
                        dve.wait_ge(logits_kept, 2 * k)
                    dve.tensor_copy(logits[:].rearrange("q j e -> q (j e)"), misc[:, 0:J * E]).then_inc(logits_ready, 1)
                if front:
                    y_means(1)
                if back:
                    wait_apart(dve, logits_ready, k + 1)
                    for j in range(J):
                        dve.max(best[:, j, :], logits[:, j, :]).then_inc(best_ready, 1)
                    for j in range(J):
                        wait_apart(dve, best_ready, J * k + j + 1)
                        dve.max_index(best_at[:, j, :], best[:, j, :], logits[:, j, :]).then_inc(best_at_ready, 1)
                    gated_inner(0)
                    dve.wait_ge(best_at_ready, J * k + J)
                    dve.tensor_tensor(chosen[:], expert_of_col[:, None, None, :].to_broadcast([P, TOP, J, E]),
                                      best_at[:, :, 0:TOP].rearrange("q j k -> q k j")[:, :, :, None].to_broadcast(
                                          [P, TOP, J, E]), ALU.is_equal).then_inc(chosen_ready, 1)
                if front:
                    y_diff(2)
                if back:
                    dve.wait_ge(chosen_ready, k + 1)
                    dve.tensor_tensor(chosen_any[:], chosen[:, 0], chosen[:, 1], ALU.add).then_inc(any_ready, 1)
                if front:
                    y_gated(2)
                    y_sum(2)
                    y_diff(3)
                    y_stats(2)
                    y_gated(3)
                    y_means(2)
                if back:
                    gated_inner(1)
                if front:
                    y_sum(3)
                if front:
                    y_stats(3)
                if back:
                    dve.wait_ge(rank_done, k + 1)
                    dve.tensor_tensor(place[:], misc[:, 0:J * E].rearrange("q (j e) -> q j e", e=E), region_of_col[:],
                                      ALU.add).then_inc(place_ready, 1)
                    dve.tensor_tensor(chosen_sum[:], chosen_sum[:], chosen_any[:], ALU.add).then_inc(sum_ready, 1)
                if front:
                    y_means(3)
                    if back:
                        dve.wait_ge(h2_ready, J * k + J)
                    if xn_next:
                        dve.wait_ge(xn_ready, J * (s + 3))
                    dve.wait_ge(ln2_moments, J * f + J)
                    if stats_next:
                        dve.wait_ge(ln1_moments, J * (s + 3) + J)

                def next_newton(m):
                    if front:
                        newton_op(s + 3, 1 - p, m)

                next_newton(0)
                next_newton(1)
                if back:
                    gated_inner(2)
                next_newton(2)
                if back:
                    dve.wait_ge(place_ready, k + 1)
                    dve.tensor_tensor(placed[:], chosen[:], place[:, None, :, :].to_broadcast([P, TOP, J, E]),
                                      ALU.mult).then_inc(placed_ready, 1)
                next_newton(3)
                if back:
                    innerT_rest(k, 0)
                next_newton(4)
                if back:
                    dve.wait_ge(placed_ready, k + 1)
                    with nc.allow_low_precision(reason="one integer below 2 ** 24 and zeros"):
                        dve.tensor_reduce(slot[:, p], placed[:], AX_X, ALU.add).then_inc(slot_ready, 1)
                next_newton(5)
                if back:
                    gated_inner(3)
                next_newton(6)
                next_newton(7)
                if back:
                    innerT_rest(k, 1)
                next_newton(8)
                if back:
                    add_shared(k, 0)
                next_newton(9)

            dve.wait_ge(const_ready, 1)
            for b in range(2):
                for j in range(J):
                    ln1_stats(b, b, 0, j)
                for j in range(J):
                    ln1_means(b, b, j, b)
                if b == 0:
                    dve.wait_ge(ln1_moments, J)
                    for m in range(NEWTON):
                        newton_op(0, 0, m)
                    dve.wait_ge(attn_w_in, W * 9)
                    steps = 0

                    def bias_link(ins):
                        nonlocal steps
                        steps += 1
                        ins.then_inc(bias_step, 1)
                        dve.wait_ge(bias_step, steps)

                    parts = [bias_thirds[:, m * 2 * D:(m + 1) * 2 * D] for m in range(3)]
                    bias_link(dve.tensor_copy(parts[0], bias_f))
                    bias_link(dve.tensor_tensor(bias_rest, bias_f, parts[0], ALU.subtract))
                    bias_link(dve.tensor_copy(parts[1], bias_rest))
                    bias_link(dve.tensor_tensor(bias_rest, bias_rest, parts[1], ALU.subtract))
                    bias_link(dve.tensor_copy(parts[2], bias_rest))
                    for m in range(3):
                        dve.tensor_copy(bias_parts[32 * m:32 * m + 1, :], parts[m][32 * m:32 * m + 1, :]).then_inc(
                            bias_ready, 1)
                    dve.wait_ge(hi_split, 5)
                    for (hi, lo), raw in ((wab, raw_wab), (wgd, raw_wgd)):
                        dve.tensor_tensor(lo[:], raw.rearrange("q (c n) -> q c n", c=KC), hi[:].bitcast(F32),
                                          ALU.subtract).then_inc(lo_split, 1)
                    dve.tensor_tensor(wc_parts[64:96, :], raw_wc[64:96, :], wc_hi[64:96, :].bitcast(F32),
                                      ALU.subtract).then_inc(lo_split, 1)
            dve.wait_ge(ln1_moments, 2 * J)
            dve.wait_ge(xn_ready, J)
            for m in range(NEWTON):
                newton_op(1, 1, m)
            dve.wait_ge(hi_split, 8)
            for (hi, lo), raw in ((wrt, raw_wrt), (wsh, raw_wsh), (wshd, raw_wshd)):
                dve.tensor_tensor(lo[:], raw.rearrange("q (c n) -> q c n", c=KC), hi[:].bitcast(F32),
                                  ALU.subtract).then_inc(lo_split, 1)
            half_steps(dve, half)

            step = 0

            def link(ins):
                nonlocal step
                step += 1
                ins.then_inc(tab_step, 1)
                dve.wait_ge(tab_step, step)

            cnt, ntile, upto, stride = (per_expert[:, m, :] for m in range(4))
            up = per_expert[:, 4, :].bitcast(I32)
            before, weighted = per_tile[:, 0], per_tile[:, 1]
            expert, row0, first = (of_tile[:, m, :] for m in range(3))
            dve.wait_ge(count_done, 1)
            link(dve.tensor_copy(cnt, misc[:, 0:E]))
            dve.tensor_tensor(fill_at[0:1, 0:E], cnt[0:1], region_of_col[0:1, 0, :], ALU.add).then_inc(fill_ready, 1)
            link(dve.tensor_scalar(up, cnt, float(P - 1), None, ALU.add))
            link(dve.tensor_scalar(up, up, 7, None, ALU.logical_shift_right))
            link(dve.tensor_copy(ntile, up))
            link(dve.tensor_scalar(stride, ntile, -float(P), float(REGION), ALU.mult, ALU.add))
            link(dve.tensor_tensor_scan(upto, ones_row[:], ntile, 0.0, ALU.mult, ALU.add))
            link(dve.tensor_tensor(before, upto[:, None, :].to_broadcast([P, 2, E]),
                                   tile_no[:, :, None].to_broadcast([P, 2, E]), ALU.is_le))
            link(dve.tensor_tensor(weighted, before, stride[:, None, :].to_broadcast([P, 2, E]), ALU.mult))
            link(dve.tensor_reduce(expert, before, AX_X, ALU.add))
            link(dve.tensor_reduce(row0, weighted, AX_X, ALU.add))
            link(dve.scalar_tensor_tensor(first, tile_no[:], float(P), row0, ALU.mult, ALU.add))
            link(dve.tensor_scalar(table_cols[:, 0:2], first, float(E * REGION), None, ALU.min))
            dve.tensor_scalar(table_cols[:, 2:4], expert, float(E - 1), float(D), ALU.min, ALU.mult).then_inc(tab_cols, 1)
            dve.wait_ge(count_done, 2)
            dve.tensor_copy(table[:], misc[0:1, :]).then_inc(tab_ready, 1)

            for e in range(0, E, 2):
                dve.wait_ge(w_hi_ready, e // 2 + 1)
                dve.tensor_tensor(w_lo[:, e:e + 2, :], raw_w[:, e:e + 2, :], w_hi[:, e:e + 2, :].bitcast(F32),
                                  ALU.subtract).then_inc(w_lo_ready, 1)

            dve.wait_ge(logits_kept, 2 * B)
            dve.tensor_tensor(all_logits[:], all_logits[:], all_best[:, :, 0:1].to_broadcast([P, NT, E]),
                              ALU.subtract).then_inc(prob_step, 1)
            dve.tensor_tensor(prob[:, 1, :], all_best[:, :, 1], all_best[:, :, 0], ALU.subtract).then_inc(prob_step, 1)

            def rows_rest(p):
                dve.tensor_tensor(bx[1][:, p, :], tr[p][:], bx[0][:, p, :].bitcast(F32), ALU.subtract).then_inc(bx_lo, 1)

            def results_out(q, w, n):
                p = w % 2
                dve.wait_ge(bdn_done, q + 1)
                if known(n, 1):
                    dve.wait_ge(by_sent[w], 2 * W * n)
                dve.tensor_copy(y[:, w], (gu, dn)[p][:].rearrange("q (h d) -> q h d", h=2)).then_inc(by_ready, 1)

            def pair(q, w, n, last=False):
                p = w % 2
                if not last:
                    dve.wait_ge(bx_hi, q + 2)
                    rows_rest(1 - p)
                if known(q, 1):
                    results_out(q - 1, (w + 3) % 4, n if w else n - 1)
                dve.wait_ge(bsilu, q + 1)
                if known(q, 2):
                    dve.wait_ge(bth_done, q - 1)
                dve.tensor_tensor(b_inner[:, p, :].rearrange("q (h f) -> q h f", h=2), gu_bank(p)[:, :, F:2 * F],
                                  b_silu[:, p, :].rearrange("q (h f) -> q h f", h=2), ALU.mult).then_inc(binner, 1)

            dve.wait_ge(bx_hi, 1)
            rows_rest(0)
            pair(0, 0, 0)
            dve.wait_ge(prob_act, 2)
            dve.tensor_reduce(prob[:, 0, :], all_logits[:], AX_X, ALU.add).then_inc(prob_step, 1)
            dve.wait_ge(prob_step, 3)
            dve.reciprocal(prob[:, 0, :], prob[:, 0, :]).then_inc(prob_step, 1)
            dve.wait_ge(prob_step, 4)
            dve.tensor_tensor(prob[:, 1, :], prob[:, 1, :], prob[:, 0, :], ALU.mult).then_inc(prob_step, 1)
            pair(1, 1, 0)
            for q in range(2, 8):
                pair(q, q % 4, q // 4)
            with dve.Fori(2, PAIRS // 4 - 1) as i:
                for w in range(4):
                    pair(4 * i + w, w, i)
            for q in range(PAIRS - 4, PAIRS):
                pair(q, q % 4, q // 4, last=q == PAIRS - 1)
            results_out(PAIRS - 1, 3, PAIRS // 4 - 1)

            def combine(b, p, n):
                dve.wait_ge(res_in[p], TOP * W * (n + 1))
                for k, done in enumerate((first_added, both_added)):
                    for j in range(J):
                        if k:
                            dve.wait_ge(first_added, J * b + j + 1)
                        tok = tokens[:, J * b + j, :]
                        dve.scalar_tensor_tensor(tok, res[:, p, k, j, :], prob[:, k, bass.ds(J * b + j, 1)], tok,
                                                 ALU.mult, ALU.add).then_inc(done, 1)

            dve.wait_ge(prob_step, 5)
            with dve.Fori(0, B // 2) as i:
                combine(2 * i, 0, i)
                combine(2 * i + 1, 1, i)

        @block.gpsimd
        def _(pool):
            steps = 0

            def link(ins):
                nonlocal steps
                steps += 1
                ins.then_inc(const_step, 1)
                wait_apart(pool, const_step, steps)

            link(pool.memset(ident[:], 0.0))
            link(pool.affine_select(out=ident[:], in_=ident[:], compare_op=ALU.not_equal, fill=1.0, base=0,
                                    pattern=[[-1, P]], channel_multiplier=1))
            link(pool.memset(ones[:], 1.0))
            link(pool.affine_select(out=earlier[:], in_=ones[:], compare_op=ALU.is_gt, fill=0.0, base=0,
                                    pattern=[[1, P]], channel_multiplier=-1))
            link(pool.memset(chosen_sum[:], 0.0))
            link(pool.memset(bias_parts[:], 0.0))
            link(pool.memset(fill_rows[:, 0:D], 0.0))
            link(pool.memset(fill_rows[:, D:ROW].bitcast(I32), NOWHERE))
            link(pool.memset(ones_row[:], 1.0))
            link(pool.iota(tile_no_i[:], pattern=[[P, 2]], base=0, channel_multiplier=1))
            link(pool.tensor_copy(tile_no[:], tile_no_i[:]))
            link(pool.memset(moments[:], 1.0))
            link(pool.memset(row_buf[:, :, :, D:ROW], 0.0))
            link(pool.memset(fill_at[:], E * REGION))
            it = slot[:].rearrange("q a k j -> q (a k j)")
            assert E <= 2 * TOP * J
            link(pool.iota(it[:, 0:E], pattern=[[1, E]], base=0, channel_multiplier=0))
            link(pool.tensor_copy(expert_of_col[:], it[:, 0:E]))
            for j in range(J):
                link(pool.tensor_scalar(region_of_col[:, j, :], expert_of_col[:], float(REGION), None, ALU.mult))
            pool.iota(result_row[:], pattern=[[P, J]], base=0, channel_multiplier=1).then_inc(const_ready, 1)

            def half(s, p, n=0):
                f, k = s + 1, s
                front, back, tail = has_front(s), has_back(s), known(s, 1)
                n_tail = (s - 1) // 2 if isinstance(s, int) else n - 1 + p

                def x_plus_dx(j):
                    wait_apart(pool, dx_ready, J * f + j + 1)
                    if known(f, 1) or j >= 2:
                        wait_apart(pool, x1_ready, J * f + j - 1)
                    pool.tensor_tensor(xdx[:, j % 2, :], tokens[:, J * f + j, :], dx[:, j % 2, :],
                                       ALU.add).then_inc(xdx_ready, 1)

                def send(q, choice, j, done):
                    pool.indirect_dma_start(
                        out=rows, out_offset=bass.IndirectOffsetOnAxis(ap=slot[:, q, choice, j:j + 1], axis=0),
                        in_=row_buf[:, q, j, :], in_offset=None).then_inc(done, W)

                if back:
                    if known(k, 2):
                        wait_apart(pool, sent2[p], W * J * n)
                    if known(k, 1):
                        wait_apart(pool, result_row_ready, k)
                    pool.tensor_copy(row_buf[:, p, :, D].bitcast(I32), result_row[:]).then_inc(first_id, 1)
                    wait_apart(pool, first_id, k + 1)
                    pool.tensor_scalar(result_row[:], result_row[:], S, None, ALU.add).then_inc(result_row_ready, 1)
                if tail:
                    wait_apart(pool, sent1[1 - p], W * J * (n_tail + 1))
                    wait_apart(pool, t2_done, 2 * k)
                    pool.tensor_scalar(row_buf[:, 1 - p, :, D].bitcast(I32), row_buf[:, 1 - p, :, D].bitcast(I32), T, None,
                                       ALU.add).then_inc(second_id, 1)
                if front:
                    x_plus_dx(0)
                if tail:
                    wait_apart(pool, second_id, k)
                    send(1 - p, 1, 0, sent2[1 - p])
                    send(1 - p, 1, 1, sent2[1 - p])
                if front:
                    x_plus_dx(1)
                if tail:
                    send(1 - p, 1, 2, sent2[1 - p])
                if front:
                    x_plus_dx(2)
                if tail:
                    send(1 - p, 1, 3, sent2[1 - p])
                if back:
                    wait_apart(pool, logits_ready, k + 1)
                    pool.tensor_copy(all_logits[:, bass.ds(J * k, J), :], logits[:]).then_inc(logits_kept, 1)
                    wait_apart(pool, best_at_ready, J * k + J)
                    pool.tensor_copy(all_best[:, bass.ds(J * k, J), :], best[:, :, 0:TOP]).then_inc(logits_kept, 1)
                if front:
                    x_plus_dx(3)
                if back:
                    wait_apart(pool, slot_ready, k + 1)
                    wait_apart(pool, h2_ready, J * k + J)
                    wait_apart(pool, first_id, k + 1)
                    for j in range(J):
                        send(p, 0, j, sent1[p])

            half_steps(pool, half)

            def keep_ids(q, w, n, at):
                wait_apart(pool, rows_in[w], 2 * W * (n + 1))
                if known(q, 8):
                    wait_apart(pool, by_sent[w], 2 * W * (n - 1))
                pool.tensor_copy(row_ids[:, at, :], row_buf[:, w // 2, 2 * (w % 2):2 * (w % 2) + 2, D].bitcast(I32)).then_inc(
                    ids_kept, 1)

            def send_pair(q, w, at):
                wait_apart(pool, by_ready, q + 1)
                wait_apart(pool, ids_kept, q + 1)
                for h in range(2):
                    pool.indirect_dma_start(
                        out=results, out_offset=bass.IndirectOffsetOnAxis(ap=row_ids[:, at, h:h + 1], axis=0),
                        in_=y[:, w, h, :], in_offset=None, bounds_check=TOP * T - 1,
                        oob_is_err=False).then_inc(by_sent[w], W)

            AHEAD = 4
            assert PAIRS % 8 == 0
            for q in range(AHEAD):
                keep_ids(q, q, 0, q)
            for q in range(8):
                keep_ids(q + AHEAD, q % 4, q // 4 + 1, (q + AHEAD) % 8)
                send_pair(q, q % 4, q)
            with pool.Fori(1, PAIRS // 8 - 1) as i:
                for m in range(8):
                    keep_ids(8 * i + m + AHEAD, m % 4, 2 * i + m // 4 + 1, (m + AHEAD) % 8)
                    send_pair(8 * i + m, m % 4, m)
            for q in range(PAIRS - 8, PAIRS):
                if q + AHEAD < PAIRS:
                    keep_ids(q + AHEAD, q % 4, q // 4 + 1, (q + AHEAD) % 8)
                send_pair(q, q % 4, q % 8)


def kernel(**inputs):
    import numpy as _np
    import concourse.bacc as _bacc
    from concourse import mybir as _mybir
    from concourse.bass_utils import run_bass_kernel_spmd as _run

    a = {k: _np.asarray(v) for k, v in inputs.items()}
    laid = {
        "x": a["L0_attn_x"],
        "wa_t": a["L0_attn_WA"].T,
        "wb_t": a["L0_attn_WB"].T,
        "wc_t": a["L0_attn_WC"].T,
        "wgd_t": _np.concatenate([a["L0_attn_Wg"].T, a["L0_attn_WD"].T], axis=1),
        "bias": _np.concatenate([a["L0_attn_bg"], a["L0_attn_bD"]])[None],
        "router_w": a["L0_ffn_router_w"],
        "gate_w": a["L0_ffn_gate_w"],
        "up_w": a["L0_ffn_up_w"],
        "down_w": a["L0_ffn_down_w"],
        "shared_gu": _np.concatenate([a["L0_ffn_shared_gate_w"], a["L0_ffn_shared_up_w"]], axis=1),
        "shared_down": a["L0_ffn_shared_down_w"],
    }
    nc = _bacc.Bacc("TRN2", target_bir_lowering=False, num_devices=1)
    arrays, args = {}, []
    for name, v in laid.items():
        v = _np.ascontiguousarray(v)
        arrays[f"in_{name}"] = v
        args.append(nc.dram_tensor(f"in_{name}", v.shape, _mybir.dt.from_np(v.dtype), kind="ExternalInput").ap())
    args.append(nc.dram_tensor("out_0", laid["x"].shape, _mybir.dt.float32, kind="ExternalOutput").ap())
    preln_gated_scan_and_routed_experts(nc, *args)
    r = _run(nc, [arrays], core_ids=[0])
    return r.results[0]["out_0"]
```

```python
from contextlib import ExitStack

import concourse.bass as bass
from concourse import mybir

ALU = mybir.AluOpType
ACT = mybir.ActivationFunctionType
AX_X = mybir.AxisListType.X
F32 = mybir.dt.float32
F32R = mybir.dt.float32r
BF16 = mybir.dt.bfloat16
I32 = mybir.dt.int32
U32 = mybir.dt.uint32

P = 128
EPS = 1e-5
RSQRT_SEED = 1597463007.0


def preln_gated_scan_and_routed_experts(nc, x, wa_t, wb_t, wc_t, wgd_t, bias, router_w, gate_w, up_w, down_w,
                                        shared_gu, shared_down, out):
    B, S, D = x.shape
    N = wa_t.shape[1]
    E = router_w.shape[1]
    F = gate_w.shape[2]
    TOP = 2
    T = B * S
    KC = D // P
    J = S // P
    NT = T // P
    TILES = TOP * NT + E
    PAIRS = TILES // 2
    REGION = T + P
    ROW = D + 4
    GU = KC * 2 * F
    NOWHERE = 2 ** 30
    W = 16
    assert D == KC * P and F == P and D == 2 * F and TOP * NT % 2 == 0 and E == B and E % 2 == 0 and TILES <= 2 * P and GU == 2 * D

    rows = nc.dram_tensor("expert_rows", (E * REGION + P, ROW), F32, kind="Internal").ap()
    results = nc.dram_tensor("expert_results", (TOP * T, D), F32, kind="Internal").ap()
    x_blocks = x.rearrange("b (j p) d -> p b j d", p=P)
    out_blocks = out.rearrange("b (j p) d -> p b j d", p=P)
    result_blocks = results.rearrange("(k b j p) d -> p k b j d", k=TOP, b=B, p=P)

    with ExitStack() as ctx:
        def sb(name, shape, dt=F32):
            return ctx.enter_context(nc.sbuf_tensor(name, shape, dt))

        def psum(name, shape, dt=F32):
            return ctx.enter_context(nc.psum_tensor(name, shape, dt))

        def sem(name):
            return ctx.enter_context(nc.semaphore(name))

        tokens = sb("tokens", [P, NT, D])
        raw_w = sb("raw_w", [P, E, GU])
        w_down = sb("w_down", [P, E, D])
        all_logits = sb("all_logits", [P, NT, E])
        all_best = sb("all_best", [P, NT, TOP])
        prob = sb("prob", [P, TOP, NT])
        ident = sb("ident", [P, P])
        row_buf = sb("row_buf", [P, 2, J, ROW])
        fill_rows = sb("fill_rows", [P, ROW])
        fill_at = sb("fill_at", [1, E], I32)
        ones_row = sb("ones_row", [P, E])
        tile_no_i = sb("tile_no_i", [P, 2], I32)
        tile_no = sb("tile_no", [P, 2])
        region_of_col = sb("region_of_col", [P, J, E])
        ones = sb("ones", [P, P], BF16)
        chosen_sum = sb("chosen_sum", [P, J, E], BF16)
        slot = sb("slot", [P, 2, TOP, J], I32)
        result_row = sb("result_row", [P, J], I32)

        part_a = ctx.enter_context(ExitStack())

        def sb_a(name, shape, dt=F32):
            return part_a.enter_context(nc.sbuf_tensor(name, shape, dt))

        wgd = [sb_a(f"wgd{a}", [P, KC, 2 * D], F32R) for a in range(2)]
        xT = [sb_a(f"xT{a}", [P, KC, S], F32R) for a in range(2)]
        xn = sb_a("xn", [P, J, D])
        wab = [sb_a(f"wab{a}", [P, KC, P], F32R) for a in range(2)]
        state_parts = sb_a("state_parts", [P, S], F32R)
        states = sb_a("states", [N, S])
        wc_parts = sb_a("wc_parts", [P, D], F32R)
        dx = sb_a("dx", [P, 2, D])
        xdx = sb_a("xdx", [P, 2, D])
        gate_t = sb_a("gate_t", [P, 2, D])
        diff = sb_a("diff", [P, 2, D])
        bias_parts = sb_a("bias_parts", [P, 2 * D], BF16)
        wsh = [sb_a(f"wsh{a}", [P, KC, 2 * D], F32R) for a in range(2)]
        h2T = [sb_a(f"h2T{a}", [P, KC, S], F32R) for a in range(2)]
        wshd = [sb_a(f"wshd{a}", [P, KC, D], F32R) for a in range(2)]
        innerT = [sb_a(f"innerT{a}", [P, 2, D], F32R) for a in range(2)]
        act_s = sb_a("act_s", [P, 2, D])
        inner = sb_a("inner", [P, 2, D])
        wrt = sb_a("wrt", [P, KC, 2 * E], F32R)
        moments = sb_a("moments", [P, 2, 2 * J, 2])
        raw1 = sb_a("raw1", [P, J, 6])
        raw2 = sb_a("raw2", [P, J, 6])
        rstd = sb_a("rstd", [P, 2 * J])
        shift = sb_a("shift", [P, 2 * J])
        half_var = sb_a("half_var", [P, 2 * J])
        newton_t = sb_a("newton_t", [P, 2 * J])
        earlier = sb_a("earlier", [P, P], BF16)
        expert_of_col = sb_a("expert_of_col", [P, E])
        logits = sb_a("logits", [P, J, E])
        best = sb_a("best", [P, J, 8])
        best_at = sb_a("best_at", [P, J, 8], U32)
        chosen = sb_a("chosen", [P, TOP, J, E])
        chosen_any = sb_a("chosen_any", [P, J, E], BF16)
        place = sb_a("place", [P, J, E])
        placed = sb_a("placed", [P, TOP, J, E])
        part_a.close()

        def staged(b, size, at=0):
            return tokens[:, J * b:J * b + J, :].rearrange("q j d -> q (j d)")[:, at:at + size]

        bias_f, bias_rest = staged(B - 1, 2 * D), staged(B - 1, 2 * D, 2 * D)
        bias_thirds = staged(B - 2, 3 * D).bitcast(BF16)
        raw_wgd, raw_wsh = staged(B - 3, 4 * D), staged(B - 4, 4 * D)
        raw_wshd, raw_wab, raw_wc = staged(B - 5, 2 * D), staged(B - 5, KC * P, 2 * D), staged(B - 5, D, 3 * D)
        raw_wrt, zeros = staged(B - 6, KC * E), staged(B - 6, S, S)
        wc_hi = h2T[0][:, 0, 0:D]

        w_hi = sb("w_hi", [P, E, GU], F32R)
        w_lo = sb("w_lo", [P, E, GU], F32R)
        bx = [sb(f"bx{a}", [P, 2, 2 * KC * P], F32R) for a in range(2)]
        b_innerT = sb("b_innerT", [P, 2, 2 * P])
        row_ids = sb("row_ids", [P, 8, 2], I32)
        late = raw_w[:].rearrange("q e w -> q (e w)")
        res = late.rearrange("q (p k j d) -> q p k j d", p=4, k=TOP, j=J)
        y = late[:, 0:8 * D].rearrange("q (w h d) -> q w h d", w=4, h=2)
        b_silu = late[:, 8 * D:8 * D + 4 * F].rearrange("q (p w) -> q p w", p=2)
        b_inner = late[:, 8 * D + 4 * F:8 * D + 8 * F].rearrange("q (p w) -> q p w", p=2)
        table = sb("table", [1, 4 * P], I32)
        per_expert = sb("per_expert", [P, 5, E])
        per_tile = sb("per_tile", [P, 2, 2, E])
        of_tile = sb("of_tile", [P, 4, 2])
        table_cols = sb("table_cols", [P, 4])

        tr = [psum(f"tr{i}", [P, 512]) for i in range(2)]
        gd = [psum(f"gd{i}", [P, 512]) for i in range(2)]
        cb = psum("cb", [P, 512])
        gu = psum("gu", [P, 512])
        dn = psum("dn", [P, 512])
        misc = psum("misc", [P, 512])

        x_in = [sem(f"x_in{i}") for i in range(2)]
        attn_w_in = sem("attn_w_in")
        ffn_w_in = sem("ffn_w_in")
        raw_w_in = sem("raw_w_in")
        stage_zeroed = sem("stage_zeroed")
        moments_set = sem("moments_set")
        attn_hi = sem("attn_hi")
        attn_lo = sem("attn_lo")
        ffn_hi = sem("ffn_hi")
        ffn_lo = sem("ffn_lo")
        const_step = sem("const_step")
        const_ready = sem("const_ready")
        bias_step = sem("bias_step")
        bias_ready = sem("bias_ready")
        w_down_in = sem("w_down_in")
        w_hi_ready = sem("w_hi_ready")
        w_lo_ready = sem("w_lo_ready")
        ln1_raw = sem("ln1_raw")
        ln1_moments = sem("ln1_moments")
        ln2_raw = sem("ln2_raw")
        ln2_moments = sem("ln2_moments")
        newton = sem("newton")
        xn_ready = sem("xn_ready")
        t1_done = sem("t1_done")
        xT_hi = sem("xT_hi")
        xT_ready = sem("xT_ready")
        ab_done = sem("ab_done")
        decay_ready = sem("decay_ready")
        scanned = sem("scanned")
        states_hi = sem("states_hi")
        states_ready = sem("states_ready")
        gd_done = sem("gd_done")
        gate_ready = sem("gate_ready")
        dx_ready = sem("dx_ready")
        xdx_ready = sem("xdx_ready")
        c_done = sem("c_done")
        diff_ready = sem("diff_ready")
        gated_ready = sem("gated_ready")
        x1_ready = sem("x1_ready")
        h2_ready = sem("h2_ready")
        t2_done = sem("t2_done")
        h2T_hi = sem("h2T_hi")
        h2T_ready = sem("h2T_ready")
        router_done = sem("router_done")
        logits_ready = sem("logits_ready")
        logits_kept = sem("logits_kept")
        best_ready = sem("best_ready")
        best_at_ready = sem("best_at_ready")
        chosen_ready = sem("chosen_ready")
        any_ready = sem("any_ready")
        rank_done = sem("rank_done")
        place_ready = sem("place_ready")
        sum_ready = sem("sum_ready")
        placed_ready = sem("placed_ready")
        slot_ready = sem("slot_ready")
        gu_done = sem("gu_done")
        silu_ready = sem("silu_ready")
        inner_ready = sem("inner_ready")
        th_done = sem("th_done")
        innerT_hi = sem("innerT_hi")
        innerT_ready = sem("innerT_ready")
        dn_done = sem("dn_done")
        shared_added = sem("shared_added")
        first_id = sem("first_id")
        result_row_ready = sem("result_row_ready")
        second_id = sem("second_id")
        sent1 = [sem(f"sent1_{i}") for i in range(2)]
        sent2 = [sem(f"sent2_{i}") for i in range(2)]
        count_done = sem("count_done")
        tab_step = sem("tab_step")
        tab_ready = sem("tab_ready")
        fill_ready = sem("fill_ready")
        filled = sem("filled")
        prob_step = sem("prob_step")
        prob_act = sem("prob_act")
        rows_in = [sem(f"rows_in{i}") for i in range(4)]
        bt_done = sem("bt_done")
        bx_hi = sem("bx_hi")
        bx_lo = sem("bx_lo")
        bgu_done = sem("bgu_done")
        bsilu = sem("bsilu")
        binner = sem("binner")
        bth_done = sem("bth_done")
        bh_ready = sem("bh_ready")
        bdn_done = sem("bdn_done")
        by_ready = sem("by_ready")
        ids_kept = sem("ids_kept")
        by_sent = [sem(f"by_sent{i}") for i in range(4)]
        res_in = [sem(f"res_in{i}") for i in range(4)]
        first_added = sem("first_added")
        both_added = sem("both_added")
        out_sent = sem("out_sent")

        NEWTON = 13
        POOL_SPLITS = 6
        PASSES = ((0, 0), (0, 1), (1, 0))
        shared_bank = (gu, tr[1])
        block = ctx.enter_context(nc.Block())

        def wait_apart(eng, semaphore, value):
            eng.wait_ge(semaphore, value)
            eng.nop(nofuse=True)

        def known(s, least):
            return not isinstance(s, int) or s >= least

        def half_steps(eng, half):
            half(-1, 1)
            for s in range(3):
                half(s, s % 2, s // 2)
            with eng.Fori(1, (B - 4) // 2) as i:
                half(2 * i + 1, 1, i)
                half(2 * i + 2, 0, i + 1)
            for s in range(B - 3, B + 1):
                half(s, s % 2, s // 2)

        def has_front(s):
            return not isinstance(s, int) or s + 1 < B

        def has_back(s):
            return not isinstance(s, int) or 0 <= s < B

        def gu_bank(p):
            return gd[p][:].rearrange("q (h w) -> q h w", h=2)

        @block.sync
        def _(sp):
            def load_x(b, p, n):
                if known(b, 2):
                    wait_apart(sp, x_in[p], W * n)
                sp.dma_start(tokens[:, bass.ds(J * b, J), :], x_blocks[:, b, :, :]).then_inc(x_in[p], W)

            def load_expert(e):
                gate_up = raw_w[:, bass.ds(e, 1), :].rearrange("q e (c g f) -> q e c g f", c=KC, g=2)[:, 0]
                sp.dma_start(gate_up[:, :, 0, :], gate_w[e].rearrange("(c q) f -> q c f", q=P)).then_inc(raw_w_in, W)
                sp.dma_start(gate_up[:, :, 1, :], up_w[e].rearrange("(c q) f -> q c f", q=P)).then_inc(raw_w_in, W)
                sp.dma_start(w_down[:, bass.ds(e, 1), :], down_w[e][:, None, :]).then_inc(w_down_in, W)

            load_x(0, 0, 0)
            sp.dma_start(raw_wgd.rearrange("q (c n) -> q c n", c=KC), wgd_t.rearrange("(c q) n -> q c n", q=P)).then_inc(
                attn_w_in, W)
            wait_apart(sp, stage_zeroed, 3)
            for q in (0, 32, 64):
                sp.dma_start(bias_f[q:q + 1, :], bias).then_inc(attn_w_in, W)
                sp.dma_start(raw_wc[q:q + N, :], wc_t).then_inc(attn_w_in, W)
            ab = raw_wab.rearrange("q (c n) -> q c n", c=KC)
            sp.dma_start(ab[:, :, 0:N], wa_t.rearrange("(c q) n -> q c n", q=P)).then_inc(attn_w_in, W)
            sp.dma_start(ab[:, :, 32:32 + N], wb_t.rearrange("(c q) n -> q c n", q=P)).then_inc(attn_w_in, W)
            load_x(1, 1, 0)
            sp.dma_start(raw_wrt.rearrange("q (c n) -> q c n", c=KC), router_w.rearrange("(c q) n -> q c n", q=P)).then_inc(
                ffn_w_in, W)
            sp.dma_start(raw_wsh.rearrange("q (c n) -> q c n", c=KC), shared_gu.rearrange("(c q) n -> q c n", q=P)).then_inc(
                ffn_w_in, W)
            sp.dma_start(raw_wshd.rearrange("q (c n) -> q c n", c=KC), shared_down.rearrange("(c q) n -> q c n", q=P)).then_inc(
                ffn_w_in, W)
            load_x(2, 0, 1)
            wait_apart(sp, attn_lo, 3)
            wait_apart(sp, ffn_lo, 3)
            wait_apart(sp, bias_ready, 3)
            with sp.Fori(0, (B - 4) // 2) as i:
                load_x(2 * i + 3, 1, i + 1)
                load_x(2 * i + 4, 0, i + 2)
                load_expert(2 * i)
                load_expert(2 * i + 1)
            load_x(B - 1, 1, B // 2 - 1)
            for e in range(B - 4, B):
                load_expert(e)

            sp.dma_start(rows[E * REGION:E * REGION + P, :], fill_rows[:]).then_inc(filled, W)
            wait_apart(sp, fill_ready, 1)
            regs = [sp.alloc_register(f"row_reg{m}") for m in range(4)]
            with sp.Fori(0, E // 4) as e:
                sp.load(regs, fill_at[0:1, bass.ds(4 * e, 4)])
                for at in [sp.snap(r, min_val=0, max_val=E * REGION) for r in regs]:
                    sp.dma_start(rows[bass.ds(at, P), :], fill_rows[:]).then_inc(filled, W)

            wait_apart(sp, filled, W * (E + 1))
            for p in range(2):
                wait_apart(sp, sent1[p], W * J * B // 2)
                wait_apart(sp, sent2[p], W * J * B // 2)
            wait_apart(sp, tab_ready, 1)

            regs += [sp.alloc_register(f"row_reg{m}") for m in range(4, 8)]

            def load_four_pairs(i):
                sp.load(regs, table[0:1, bass.ds(8 * i, 8)])
                at = [sp.snap(r, min_val=0, max_val=E * REGION) for r in regs]
                for b in range(8):
                    if b % 4 == 0 and known(i, 1):
                        wait_apart(sp, ids_kept, 4 * i - 2 + b // 2)
                    sp.dma_start(row_buf[:, b // J, b % J, :], rows[bass.ds(at[b], P), :]).then_inc(rows_in[b // 2], W)

            assert PAIRS % 4 == 0
            load_four_pairs(0)
            with sp.Fori(1, PAIRS // 4) as i:
                load_four_pairs(i)

            for w in range(4):
                wait_apart(sp, by_sent[w], W * 2 * PAIRS // 4)
            wait_apart(sp, tab_ready, 1)

            def load_results(b, w, n):
                if known(n, 1):
                    wait_apart(sp, both_added, J * b - 3 * J)
                for k in range(TOP):
                    sp.dma_start(res[:, w, k], result_blocks[:, k, b, :, :]).then_inc(res_in[w], W)

            for w in range(4):
                load_results(w, w, 0)
            with sp.Fori(1, B // 4) as i:
                for w in range(4):
                    load_results(4 * i + w, w, i)
            wait_apart(sp, out_sent, W * B)

        @block.tensor
        def _(pe):
            def transposes(bank, at, src, sem_, n=1):
                for k, s in enumerate(src):
                    last = pe.transpose(bank[:, at + P * k:at + P * k + P], s, ident[:])
                last.then_inc(sem_, n)

            def three_passes(dst, lhs, rhs):
                steps = [(a, b, c) for a, b in PASSES for c in range(KC)]
                for m, (a, b, c) in enumerate(steps):
                    last = pe.matmul(dst, lhs(a, c), rhs(b, c), start=m == 0, stop=m == len(steps) - 1)
                return last

            def shared_down_of(k, j):
                pe.wait_ge(innerT_ready, J * k + j + 1)
                if known(k, 1) or j:
                    pe.wait_ge(shared_added, J * k + j)
                three_passes(dn[:, 0:D], lambda a, c: innerT[a][:, j % 2, c * P:(c + 1) * P],
                             lambda b, c: wshd[b][:, c, :]).then_inc(dn_done, 1)

            def inner_transposes(k, j):
                pe.wait_ge(inner_ready, J * k + j + 1)
                if j:
                    pe.wait_ge(innerT_ready, J * k + j)
                transposes(cb, 0, [inner[:, j % 2, c * P:(c + 1) * P] for c in range(KC)], th_done)

            def front_transposes(b, g):
                pe.wait_ge(xn_ready, J * b + 2 * g + 2)
                transposes(tr[g], 0, [xn[:, 2 * g + h, c * P:(c + 1) * P] for h in range(2) for c in range(KC)], t1_done)

            def half(s, p, n=0):
                f, k = s + 1, s
                front, back, tail = has_front(s), has_back(s), known(s, 1)
                last_back = isinstance(s, int) and s == B - 1
                xn_next = not isinstance(s, int) or s + 2 < B

                def gate_and_dx(j):
                    if known(f, 1) or j >= 2:
                        pe.wait_ge(dx_ready, J * f + j - 1)
                    for a, b in PASSES:
                        for c in range(KC):
                            pe.matmul(gd[j % 2][:], xT[a][:, c, j * P:(j + 1) * P], wgd[b][:, c, :],
                                      start=(a, b, c) == (0, 0, 0), stop=False)
                    pe.matmul(gd[j % 2][:], ones[:], bias_parts[:], start=False, stop=True).then_inc(gd_done, 1)

                def recurrent(j):
                    if known(f, 1) or j:
                        pe.wait_ge(diff_ready, J * f + j)
                    pe.matmul(cb[:, 0:D], state_parts[0:96, j * P:(j + 1) * P], wc_parts[0:96, :],
                              start=True, stop=True).then_inc(c_done, 1)

                def ranks_of_block():
                    pe.wait_ge(any_ready, k + 1)
                    ranks = misc[:, 0:J * E].rearrange("q (j e) -> q j e", e=E)
                    pe.matmul(ranks, earlier[:], chosen_any[:], start=True, stop=False)
                    for j in range(J - 1):
                        pe.matmul(ranks[:, j + 1:J, :], ones[:],
                                  chosen_any[:, j:j + 1, :].to_broadcast([P, J - 1 - j, E]), start=False, stop=False)
                    for j in range(J):
                        last = pe.matmul(ranks, ones[:], chosen_sum[:, j:j + 1, :].to_broadcast([P, J, E]),
                                         start=False, stop=j == J - 1)
                    last.then_inc(rank_done, 1)

                def shared_gate_up(j):
                    if known(k, 1) or j >= 2:
                        pe.wait_ge(inner_ready, J * k + j - 1)
                    three_passes(shared_bank[j % 2][:], lambda a, c: h2T[a][:, c, j * P:(j + 1) * P],
                                 lambda b, c: wsh[b][:, c, :]).then_inc(gu_done, 1)

                if front:
                    if isinstance(s, int) and s == -1:
                        pe.wait_ge(attn_lo, 3)
                        pe.wait_ge(bias_ready, 3)
                    pe.wait_ge(xT_ready, 2 * f + 1)
                    gate_and_dx(0)
                if tail:
                    inner_transposes(k - 1, 2)
                if front and known(s, 0):
                    if tail:
                        pe.wait_ge(inner_ready, J * k)
                    else:
                        pe.wait_ge(xT_ready, 2 * f)
                    front_transposes(f, 1)
                if tail:
                    shared_down_of(k - 1, 1)
                    inner_transposes(k - 1, 3)
                    shared_down_of(k - 1, 2)
                if front:
                    pe.wait_ge(xT_ready, 2 * f + 2)
                    if tail:
                        pe.wait_ge(place_ready, k)
                    elif known(k, 0):
                        pe.wait_ge(scanned, f)
                    three_passes(misc[:], lambda a, c: wab[a][:, c, :], lambda b, c: xT[b][:, c, :]).then_inc(ab_done, 1)
                def back_transposes(g):
                    pe.wait_ge(h2_ready, J * k + 2 * g + 2)
                    if front:
                        pe.wait_ge(xT_ready, 2 * f + g + 1)
                    elif g == 0:
                        pe.wait_ge(h2T_ready, 2 * k - 1)
                    else:
                        pe.wait_ge(inner_ready, J * k)
                    transposes(tr[g], 0, [row_buf[:, p, 2 * g + h, c * P:(c + 1) * P]
                                          for h in range(2) for c in range(KC)], t2_done)

                if front:
                    gate_and_dx(1)
                if back:
                    back_transposes(0)
                if tail:
                    shared_down_of(k - 1, 3)
                if back:
                    back_transposes(1)
                if front:
                    pe.wait_ge(states_ready, f + 1)
                    pe.wait_ge(states_hi, 2 * f + 2)
                    if tail:
                        pe.wait_ge(innerT_ready, J * k)
                    recurrent(0)
                    gate_and_dx(2)
                    recurrent(1)
                if back:
                    pe.wait_ge(h2T_ready, 2 * k + 2)
                    if last_back:
                        pe.wait_ge(place_ready, k)
                    if isinstance(s, int) and s == 0:
                        pe.wait_ge(ffn_lo, 3)
                    for j in range(J):
                        for a in range(2):
                            for c in range(KC):
                                last = pe.matmul(misc[:, j * 2 * E:(j + 1) * 2 * E], h2T[a][:, c, j * P:(j + 1) * P],
                                                 wrt[:, c, :], start=a == c == 0, stop=a == 1 and c == KC - 1)
                    last.then_inc(router_done, 1)
                    shared_gate_up(0)
                    if not front:
                        ranks_of_block()
                if front:
                    recurrent(2)
                    gate_and_dx(3)
                if back:
                    shared_gate_up(1)
                if last_back:
                    pe.wait_ge(sum_ready, B)
                    for j in range(J):
                        last = pe.matmul(misc[:, 0:E], ones[:], chosen_sum[:, j, :], start=j == 0, stop=j == J - 1)
                    last.then_inc(count_done, 1)
                if front:
                    recurrent(3)
                if back:
                    if front:
                        ranks_of_block()
                    shared_gate_up(2)
                    if front:
                        pe.wait_ge(diff_ready, J * f + J)
                    else:
                        pe.wait_ge(innerT_ready, J * k)
                    inner_transposes(k, 0)
                if xn_next:
                    if back:
                        pe.wait_ge(h2T_ready, 2 * k + 1)
                    else:
                        pe.wait_ge(xT_ready, 2 * f + 1)
                    front_transposes(s + 2, 0)
                if back:
                    shared_gate_up(3)
                    inner_transposes(k, 1)
                    shared_down_of(k, 0)

            pe.wait_ge(const_ready, 1)
            front_transposes(0, 0)
            front_transposes(0, 1)
            half_steps(pe, half)

            pe.wait_ge(tab_step, 13)
            for c in range(4):
                last = pe.matmul(misc[0:1, c * P:(c + 1) * P], table_cols[:, c:c + 1], ident[:],
                                 start=True, stop=True)
            last.then_inc(count_done, 1)

            gate_up_w = [w[:].rearrange("q e w -> q (e w)") for w in (w_hi, w_lo)]
            down_w_flat = w_down[:].rearrange("q e d -> q (e d)")
            btr, bgu, bth, bdn = (tr[0], tr[1]), (gd[0], gd[1]), cb, (gu, dn)
            regs = [pe.alloc_register(f"weight_reg{k}") for k in range(6)]

            def rows_transposed(q, w, p, n):
                pe.wait_ge(rows_in[w], 2 * W * (n + 1))
                if known(q, 2):
                    pe.wait_ge(bx_lo, q - 1)
                srcs = [row_buf[:, (2 * w + h) // J, (2 * w + h) % J, c * P:(c + 1) * P]
                        for h in range(2) for c in range(KC)]
                transposes(btr[p], 0, srcs, bt_done)

            def gate_up(q, p, at):
                pe.wait_ge(bx_lo, q + 1)
                if known(q, 2):
                    pe.wait_ge(binner, q - 1)
                for h in range(2):
                    steps = [(a, b, c) for a, b in PASSES for c in range(KC)]
                    for m, (a, b, c) in enumerate(steps):
                        last = pe.matmul(bgu[p][:, h * 2 * F:(h + 1) * 2 * F],
                                         bx[a][:, p, (h * KC + c) * P:(h * KC + c + 1) * P],
                                         gate_up_w[b][:, bass.ds(at[h] * 2 + c * 2 * F, 2 * F)],
                                         start=m == 0, stop=m == len(steps) - 1)
                last.then_inc(bgu_done, 1)

            def inner_turned(q, p):
                pe.wait_ge(binner, q + 1)
                if known(q, 1):
                    pe.wait_ge(bh_ready, q)
                transposes(bth, 0, [b_inner[:, p, h * F:(h + 1) * F] for h in range(2)], bth_done)

            def down(q, p, at):
                pe.wait_ge(bh_ready, q + 1)
                if known(q, 2):
                    pe.wait_ge(by_ready, q - 1)
                for h in range(2):
                    last = pe.matmul(bdn[p][:, h * D:(h + 1) * D], b_innerT[:, p, h * P:(h + 1) * P],
                                     down_w_flat[:, bass.ds(at[h], D)], start=True, stop=True)
                last.then_inc(bdn_done, 1)

            def weight_at(first, count):
                use = regs[:count]
                pe.load(use, table[0:1, bass.ds(first, count)])
                return [pe.snap(r, min_val=0, max_val=(E - 1) * D) for r in use]

            pe.wait_ge(tab_ready, 1)
            rows_transposed(0, 0, 0, 0)
            at = weight_at(2 * P, 4)
            rows_transposed(1, 1, 1, 0)
            pe.wait_ge(w_lo_ready, E // 2)
            pe.wait_ge(w_down_in, W * E)
            gate_up(0, 0, at[0:2])
            rows_transposed(2, 2, 0, 0)
            inner_turned(0, 0)
            gate_up(1, 1, at[2:4])
            down(0, 0, at[0:2])

            def two_pairs(q, w, n, last=False):
                at = weight_at(2 * q + 2 * P - 2, 6)
                rows_transposed(q + 1, w + 1, 1, n)
                inner_turned(q - 1, 1)
                gate_up(q, 0, at[2:4])
                down(q - 1, 1, at[0:2])
                if not last:
                    rows_transposed(q + 2, (w + 2) % 4, 0, n + (w == 2))
                inner_turned(q, 0)
                gate_up(q + 1, 1, at[4:6])
                down(q, 0, at[2:4])

            two_pairs(2, 2, 0)
            with pe.Fori(1, PAIRS // 4 - 1) as i:
                two_pairs(4 * i, 0, i)
                two_pairs(4 * i + 2, 2, i)
            two_pairs(PAIRS - 4, 0, PAIRS // 4 - 1)
            two_pairs(PAIRS - 2, 2, PAIRS // 4 - 1, last=True)
            at = weight_at(2 * P + TILES - 2, 2)
            inner_turned(PAIRS - 1, 1)
            down(PAIRS - 1, 1, at)

        @block.scalar
        def _(act):
            def normalise(dst, b, j, col, done):
                act.activation(dst, tokens[:, J * b + j, :], ACT.Identity, scale=rstd[:, col:col + 1],
                               bias=shift[:, col:col + 1]).then_inc(done, 1)

            def turned_out(dst, bank, g, done):
                act.activation(dst[:, :, g * 2 * P:(g + 1) * 2 * P].rearrange("q c (h t) -> q h c t", h=2),
                               bank[:].rearrange("q (h c t) -> q h c t", h=2, c=KC), ACT.Copy).then_inc(done, 1)

            def innerT_out(k, j):
                act.wait_ge(th_done, J * k + j + 1)
                if known(k, 1) or j >= 2:
                    act.wait_ge(dn_done, J * k + j - 1)
                act.activation(innerT[0][:, j % 2, :], cb[:, 0:D], ACT.Copy).then_inc(innerT_hi, 1)

            def half(s, p, n=0):
                f, k = s + 1, s
                front, back, tail = has_front(s), has_back(s), known(s, 1)
                last_back = isinstance(s, int) and s == B - 1
                xn_next = not isinstance(s, int) or s + 2 < B

                def expert_hi(count):
                    nonlocal pairs_split
                    if last_back:
                        for m in range(pairs_split, pairs_split + count):
                            act.activation(w_hi[:, 2 * m:2 * m + 2, :], raw_w[:, 2 * m:2 * m + 2, :], ACT.Copy).then_inc(
                                w_hi_ready, 1)
                        pairs_split += count

                pairs_split = 0

                def gate_and_dx_out(j):
                    act.wait_ge(gd_done, J * f + j + 1)
                    if known(f, 1) or j >= 2:
                        act.wait_ge(gated_ready, J * f + j - 1)
                        act.wait_ge(xdx_ready, J * f + j - 1)
                    act.activation(gate_t[:, j % 2, :], gd[j % 2][:, 0:D], ACT.Tanh, scale=0.5).then_inc(gate_ready, 1)
                    act.activation(dx[:, j % 2, :], gd[j % 2][:, D:2 * D], ACT.Copy).then_inc(dx_ready, 1)

                def silu_out(j):
                    act.wait_ge(gu_done, J * k + j + 1)
                    if known(k, 1) or j >= 2:
                        act.wait_ge(inner_ready, J * k + j - 1)
                    act.activation(act_s[:, j % 2, :], shared_bank[j % 2][:, 0:D], ACT.Silu).then_inc(silu_ready, 1)

                if tail:
                    innerT_out(k - 1, 2)
                if front:
                    gate_and_dx_out(0)
                if front and known(s, 0):
                    act.wait_ge(t1_done, 2 * f + 2)
                    turned_out(xT[0], tr[1], 1, xT_hi)
                if tail:
                    innerT_out(k - 1, 3)

                def h2(j):
                    normalise(row_buf[:, p, j, 0:D], k, j, j, h2_ready)

                if back:
                    act.wait_ge(newton, NEWTON * (s + 3))
                    if known(k, 2):
                        act.wait_ge(sent2[p], W * J * n)
                    h2(0)
                    h2(1)
                if front:
                    act.wait_ge(ab_done, f + 1)
                    if known(f, 1):
                        act.wait_ge(states_ready, f)
                        act.wait_ge(states_hi, 2 * f)
                    act.activation(states[:], misc[0:N, :], ACT.Tanh).then_inc(decay_ready, 1)
                if back:
                    h2(2)
                    h2(3)
                if front:
                    act.wait_ge(scanned, f + 1)
                    if known(f, 1):
                        act.wait_ge(c_done, J * f)
                    for q in (0, 64):
                        act.activation(state_parts[q:q + N, :], states[:], ACT.Copy).then_inc(states_hi, 1)
                if back:
                    if known(k, 1):
                        act.wait_ge(gu_done, J * k)
                    for g in range(2):
                        act.wait_ge(t2_done, 2 * k + g + 1)
                        turned_out(h2T[0], tr[g], g, h2T_hi)
                if front:
                    gate_and_dx_out(1)
                    gate_and_dx_out(2)
                if xn_next:
                    act.wait_ge(newton, NEWTON * (s + 3))
                    act.wait_ge(t1_done, 2 * f + 2)
                    for j in range(J):
                        normalise(xn[:, j, :], s + 2, j, J + j, xn_ready)
                if last_back:
                    act.wait_ge(raw_w_in, 2 * W * E)
                    act.wait_ge(c_done, J * B)
                    act.wait_ge(ln2_moments, J * B)
                expert_hi(3)
                if back:
                    silu_out(0)
                expert_hi(1)
                if front:
                    gate_and_dx_out(3)
                if back:
                    silu_out(1)
                expert_hi(1)
                if back:
                    silu_out(2)
                    innerT_out(k, 0)
                if xn_next:
                    act.wait_ge(gd_done, J * f + J)
                    act.wait_ge(t1_done, 2 * (s + 2) + 1)
                    turned_out(xT[0], tr[0], 0, xT_hi)
                if back:
                    silu_out(3)
                    innerT_out(k, 1)
                expert_hi(3)

            act.wait_ge(attn_w_in, W * 9)
            act.wait_ge(stage_zeroed, 4)
            act.activation(wab[0][:], raw_wab.rearrange("q (c n) -> q c n", c=KC), ACT.Copy).then_inc(attn_hi, 1)
            act.activation(wgd[0][:], raw_wgd.rearrange("q (c n) -> q c n", c=KC), ACT.Copy).then_inc(attn_hi, 1)
            act.activation(wc_hi, raw_wc, ACT.Copy).then_inc(attn_hi, 1)
            act.activation(wc_parts[0:64, :], raw_wc[0:64, :], ACT.Copy).then_inc(attn_hi, 1)
            act.activation(state_parts[:], zeros, ACT.Copy).then_inc(attn_hi, 1)
            act.wait_ge(newton, NEWTON)
            act.wait_ge(x_in[0], W)
            for j in range(J):
                normalise(xn[:, j, :], 0, j, J + j, xn_ready)
            for g in range(2):
                act.wait_ge(t1_done, g + 1)
                turned_out(xT[0], tr[g], g, xT_hi)
            act.wait_ge(ffn_w_in, W * 3)
            act.wait_ge(attn_hi, 5)
            act.wait_ge(attn_lo, 3)
            act.activation(wsh[0][:], raw_wsh.rearrange("q (c n) -> q c n", c=KC), ACT.Copy).then_inc(ffn_hi, 1)
            act.activation(wshd[0][:], raw_wshd.rearrange("q (c n) -> q c n", c=KC), ACT.Copy).then_inc(ffn_hi, 1)
            act.activation(wrt[:, :, 0:E], raw_wrt.rearrange("q (c n) -> q c n", c=KC), ACT.Copy).then_inc(ffn_hi, 1)
            half_steps(act, half)

            def inner_turned_out(q, p):
                act.wait_ge(bth_done, q + 1)
                if known(q, 2):
                    act.wait_ge(bdn_done, q - 1)
                act.activation(b_innerT[:, p, :], cb[:, 0:2 * F], ACT.Copy).then_inc(bh_ready, 1)

            def pair(q, p, last=False):
                if not last:
                    act.wait_ge(bt_done, q + 2)
                    if known(q, 1):
                        act.wait_ge(bgu_done, q)
                    act.activation(bx[0][:, 1 - p, :], tr[1 - p][:], ACT.Copy).then_inc(bx_hi, 1)
                if known(q, 1):
                    inner_turned_out(q - 1, 1 - p)
                act.wait_ge(bgu_done, q + 1)
                if known(q, 2):
                    act.wait_ge(binner, q - 1)
                act.activation(b_silu[:, p, :].rearrange("q (h f) -> q h f", h=2),
                               gu_bank(p)[:, :, 0:F], ACT.Silu).then_inc(bsilu, 1)

            act.wait_ge(bt_done, 1)
            act.activation(bx[0][:, 0, :], tr[0][:], ACT.Copy).then_inc(bx_hi, 1)
            pair(0, 0)
            pair(1, 1)
            pair(2, 0)
            pair(3, 1)
            with act.Fori(2, PAIRS // 2 - 1) as i:
                pair(2 * i, 0)
                pair(2 * i + 1, 1)
            pair(PAIRS - 2, 0)
            pair(PAIRS - 1, 1, last=True)
            inner_turned_out(PAIRS - 1, 1)

            act.wait_ge(prob_step, 2)
            act.activation(all_logits[:], all_logits[:], ACT.Exp).then_inc(prob_act, 1)
            act.activation(prob[:, 1, :], prob[:, 1, :], ACT.Exp).then_inc(prob_act, 1)

            with act.Fori(0, B) as b:
                act.wait_ge(both_added, J * b + J)
                act.dma_start(out_blocks[:, b, :, :], tokens[:, bass.ds(J * b, J), :]).then_inc(out_sent, W)

        @block.vector
        def _(dve):
            dve.memset(raw_wab, 0.0).then_inc(stage_zeroed, 1)
            dve.memset(staged(B - 5, D, 3 * D), 0.0).then_inc(stage_zeroed, 1)
            dve.memset(staged(B - 1, 4 * D), 0.0).then_inc(stage_zeroed, 1)
            dve.memset(zeros, 0.0).then_inc(stage_zeroed, 1)
            dve.memset(moments[:], 1.0).then_inc(moments_set, 1)
            dve.memset(bias_parts[:], 0.0).then_inc(bias_step, 1)

            def ln1_stats(b, p, n, j):
                if j == 0:
                    dve.wait_ge(x_in[p], W * (n + 1))
                if known(b, 1):
                    wait_apart(dve, ln1_moments, J * b - J + j + 1)
                dve.bn_stats(raw1[:, j, :], tokens[:, J * b + j, :]).then_inc(ln1_raw, 1)

            def ln1_means(b, p, j, m):
                wait_apart(dve, ln1_raw, J * b + j + 1)
                dve.bn_aggr(moments[:, m, J + j, :], raw1[:, j, :]).then_inc(ln1_moments, 1)

            def newton_op(h, p, m):
                mean, var = moments[:, p, :, 0], moments[:, p, :, 1]
                if m >= 2:
                    dve.wait_ge(newton, NEWTON * h + m)
                if m == 0:
                    ins = dve.tensor_scalar(half_var[:], var, -0.5, -0.5 * EPS, ALU.mult, ALU.add)
                elif m == 1:
                    ins = dve.tensor_scalar(newton_t[:], var, EPS, None, ALU.add)
                elif m == 2:
                    ins = dve.tensor_scalar(rstd[:].bitcast(I32), newton_t[:].bitcast(I32), -0.5, RSQRT_SEED,
                                            ALU.mult, ALU.add)
                elif m == NEWTON - 1:
                    ins = dve.scalar_tensor_tensor(shift[:], mean, -1.0, rstd[:], ALU.mult, ALU.mult)
                elif m % 3 == 0:
                    ins = dve.tensor_tensor(newton_t[:], rstd[:], rstd[:], ALU.mult)
                elif m % 3 == 1:
                    ins = dve.tensor_tensor(newton_t[:], newton_t[:], half_var[:], ALU.mult)
                else:
                    ins = dve.scalar_tensor_tensor(rstd[:], newton_t[:], 1.5, rstd[:], ALU.add, ALU.mult)
                ins.then_inc(newton, 1)

            cnt, ntile, upto, stride = (per_expert[:, m, :] for m in range(4))
            up = per_expert[:, 4, :].bitcast(I32)
            before, weighted = per_tile[:, 0], per_tile[:, 1]
            expert, row0, first = (of_tile[:, m, :] for m in range(3))
            table_steps = (
                lambda: dve.tensor_copy(cnt, misc[:, 0:E]),
                lambda: dve.tensor_scalar(up, cnt, float(P - 1), None, ALU.add),
                lambda: dve.tensor_scalar(up, up, 7, None, ALU.logical_shift_right),
                lambda: dve.tensor_copy(ntile, up),
                lambda: dve.tensor_scalar(stride, ntile, -float(P), float(REGION), ALU.mult, ALU.add),
                lambda: dve.tensor_tensor_scan(upto, ones_row[:], ntile, 0.0, ALU.mult, ALU.add),
                lambda: dve.tensor_tensor(before, upto[:, None, :].to_broadcast([P, 2, E]),
                                          tile_no[:, :, None].to_broadcast([P, 2, E]), ALU.is_le),
                lambda: dve.tensor_tensor(weighted, before, stride[:, None, :].to_broadcast([P, 2, E]), ALU.mult),
                lambda: dve.tensor_reduce(expert, before, AX_X, ALU.add),
                lambda: dve.tensor_reduce(row0, weighted, AX_X, ALU.add),
                lambda: dve.scalar_tensor_tensor(first, tile_no[:], float(P), row0, ALU.mult, ALU.add),
                lambda: dve.tensor_scalar(table_cols[:, 0:2], first, float(E * REGION), None, ALU.min),
                lambda: dve.tensor_scalar(table_cols[:, 2:4], expert, float(E - 1), float(D), ALU.min, ALU.mult))

            def steps_to_table(s, at, end):
                if isinstance(s, int) and s == B:
                    for m in range(at, end):
                        if m:
                            dve.wait_ge(tab_step, m)
                        table_steps[m]().then_inc(tab_step, 1)

            def innerT_rest(k, j):
                dve.wait_ge(innerT_hi, J * k + j + 1)
                dve.tensor_tensor(innerT[1][:, j % 2, :], cb[:, 0:D], innerT[0][:, j % 2, :].bitcast(F32),
                                  ALU.subtract).then_inc(innerT_ready, 1)

            def turned_rest(dst, bank, g):
                at = slice(g * 2 * P, (g + 1) * 2 * P)
                return dve.tensor_tensor(dst[1][:, :, at].rearrange("q c (h t) -> q h c t", h=2),
                                         bank[:].rearrange("q (h c t) -> q h c t", h=2, c=KC),
                                         dst[0][:, :, at].rearrange("q c (h t) -> q h c t", h=2).bitcast(F32), ALU.subtract)

            def add_shared(k, j):
                dve.wait_ge(dn_done, J * k + j + 1)
                dve.tensor_tensor(tokens[:, J * k + j, :], tokens[:, J * k + j, :], dn[:, 0:D],
                                  ALU.add).then_inc(shared_added, 1)

            def half(s, p, n=0):
                f, k = s + 1, s
                front, back, tail = has_front(s), has_back(s), known(s, 1)
                last_back = isinstance(s, int) and s == B - 1
                stats_next = not isinstance(s, int) or s + 3 < B
                xn_next = not isinstance(s, int) or s + 2 < B
                n3 = (s + 3) // 2 if isinstance(s, int) else n + 1 + p

                def y_diff(j):
                    dve.wait_ge(c_done, J * f + j + 1)
                    dve.wait_ge(dx_ready, J * f + j + 1)
                    dve.tensor_tensor(diff[:, j % 2, :], cb[:, 0:D], dx[:, j % 2, :], ALU.subtract).then_inc(diff_ready, 1)

                def y_gated(j):
                    dve.wait_ge(gate_ready, J * f + j + 1)
                    dve.wait_ge(diff_ready, J * f + j + 1)
                    dve.scalar_tensor_tensor(diff[:, j % 2, :], gate_t[:, j % 2, :], 1.0, diff[:, j % 2, :],
                                             ALU.add, ALU.mult).then_inc(gated_ready, 1)

                def y_sum(j):
                    dve.wait_ge(gated_ready, J * f + j + 1)
                    dve.wait_ge(xdx_ready, J * f + j + 1)
                    dve.scalar_tensor_tensor(tokens[:, J * f + j, :], diff[:, j % 2, :], 0.5, xdx[:, j % 2, :],
                                             ALU.mult, ALU.add).then_inc(x1_ready, 1)

                def y_stats(j):
                    dve.wait_ge(x1_ready, J * f + j + 1)
                    if known(f, 1):
                        wait_apart(dve, ln2_moments, J * f - J + j + 1)
                    dve.bn_stats(raw2[:, j, :], tokens[:, J * f + j, :]).then_inc(ln2_raw, 1)

                def y_means(j):
                    wait_apart(dve, ln2_raw, J * f + j + 1)
                    dve.bn_aggr(moments[:, 1 - p, j, :], raw2[:, j, :]).then_inc(ln2_moments, 1)

                def gated_inner(j):
                    dve.wait_ge(silu_ready, J * k + j + 1)
                    if known(k, 1) or j >= 2:
                        dve.wait_ge(th_done, J * k + j - 1)
                    dve.tensor_tensor(inner[:, j % 2, :], shared_bank[j % 2][:, D:2 * D], act_s[:, j % 2, :],
                                      ALU.mult).then_inc(inner_ready, 1)

                def stats(j):
                    if stats_next:
                        ln1_stats(s + 3, 1 - p, n3, j)

                def means(j):
                    if stats_next:
                        ln1_means(s + 3, 1 - p, j, 1 - p)

                def places():
                    dve.wait_ge(rank_done, k + 1)
                    dve.tensor_tensor(place[:], misc[:, 0:J * E].rearrange("q (j e) -> q j e", e=E), region_of_col[:],
                                      ALU.add).then_inc(place_ready, 1)

                def count():
                    dve.tensor_tensor(chosen_sum[:], chosen_sum[:], chosen_any[:], ALU.add).then_inc(sum_ready, 1)

                def places_chosen():
                    dve.wait_ge(place_ready, k + 1)
                    dve.tensor_tensor(placed[:], chosen[:], place[:, None, :, :].to_broadcast([P, TOP, J, E]),
                                      ALU.mult).then_inc(placed_ready, 1)

                def slots():
                    dve.wait_ge(placed_ready, k + 1)
                    with nc.allow_low_precision(reason="one integer below 2 ** 24 and zeros"):
                        dve.tensor_reduce(slot[:, p], placed[:], AX_X, ALU.add).then_inc(slot_ready, 1)

                if back:
                    newton_op(s + 2, p, 8)
                if tail:
                    innerT_rest(k - 1, 2)
                steps_to_table(s, 0, 4)
                if back:
                    newton_op(s + 2, p, 9)
                if tail:
                    add_shared(k - 1, 1)
                steps_to_table(s, 4, 7)
                if back:
                    newton_op(s + 2, p, 10)
                if front and known(s, 0):
                    dve.wait_ge(xT_hi, 2 * f + 2)
                    turned_rest(xT, tr[1], 1).then_inc(xT_ready, 1)
                if isinstance(s, int) and s == -1:
                    dve.wait_ge(ln1_moments, 2 * J)
                    dve.wait_ge(xn_ready, J)
                    for m in range(NEWTON):
                        newton_op(1, 1, m)
                if back:
                    newton_op(s + 2, p, 11)
                if tail:
                    innerT_rest(k - 1, 3)
                steps_to_table(s, 7, 11)
                if back:
                    newton_op(s + 2, p, 12)
                stats(0)
                if tail:
                    add_shared(k - 1, 2)
                steps_to_table(s, 11, 13)
                stats(1)
                if front:
                    dve.wait_ge(decay_ready, f + 1)
                    dve.tensor_tensor_scan(states[:], states[:], misc[32:32 + N, :], 0.0,
                                           ALU.mult, ALU.add).then_inc(scanned, 1)
                stats(2)
                means(0)
                means(1)
                if front:
                    dve.wait_ge(states_hi, 2 * f + 1)
                    dve.tensor_tensor(state_parts[32:32 + N, :], states[:], state_parts[0:N, :].bitcast(F32),
                                      ALU.subtract).then_inc(states_ready, 1)
                stats(3)
                means(2)
                if back:
                    dve.wait_ge(h2T_hi, 2 * k + 1)
                    turned_rest(h2T, tr[0], 0).then_inc(h2T_ready, 1)
                if front:
                    y_diff(0)
                if back:
                    dve.wait_ge(h2T_hi, 2 * k + 2)
                    turned_rest(h2T, tr[1], 1).then_inc(h2T_ready, 1)
                means(3)
                if front:
                    y_gated(0)
                if tail:
                    add_shared(k - 1, 3)
                if front:
                    y_sum(0)
                    y_diff(1)
                    y_stats(0)
                    y_gated(1)
                    y_means(0)
                    y_sum(1)
                    y_stats(1)
                if back:
                    dve.wait_ge(router_done, k + 1)
                    if known(k, 1):
                        dve.wait_ge(logits_kept, 2 * k)
                    both = misc[:, 0:J * 2 * E].rearrange("q (j a e) -> q j e a", a=2, e=E)
                    dve.tensor_reduce(logits[:], both, AX_X, ALU.add).then_inc(logits_ready, 1)
                if front:
                    y_means(1)
                if back:
                    wait_apart(dve, logits_ready, k + 1)
                    for j in range(J):
                        dve.max(best[:, j, :], logits[:, j, :]).then_inc(best_ready, 1)
                    for j in range(J):
                        wait_apart(dve, best_ready, J * k + j + 1)
                        dve.max_index(best_at[:, j, :], best[:, j, :], logits[:, j, :]).then_inc(best_at_ready, 1)
                    if not last_back:
                        gated_inner(0)
                if front:
                    y_diff(2)
                if back:
                    dve.wait_ge(best_at_ready, J * k + J)
                    dve.tensor_tensor(chosen[:], expert_of_col[:, None, None, :].to_broadcast([P, TOP, J, E]),
                                      best_at[:, :, 0:TOP].rearrange("q j k -> q k j")[:, :, :, None].to_broadcast(
                                          [P, TOP, J, E]), ALU.is_equal).then_inc(chosen_ready, 1)
                if front:
                    y_gated(2)
                if back:
                    dve.wait_ge(chosen_ready, k + 1)
                    dve.tensor_tensor(chosen_any[:], chosen[:, 0], chosen[:, 1], ALU.add).then_inc(any_ready, 1)
                if front:
                    y_sum(2)
                if last_back:
                    gated_inner(0)
                    places()
                    count()
                    places_chosen()
                    slots()
                if last_back:
                    dve.wait_ge(count_done, 1)
                    dve.tensor_tensor(fill_at[:], misc[0:1, 0:E], region_of_col[0:1, 0, :], ALU.add).then_inc(fill_ready, 1)
                if back:
                    gated_inner(1)
                if front:
                    y_diff(3)
                    y_stats(2)
                    y_gated(3)
                    y_means(2)
                    y_sum(3)
                if back:
                    gated_inner(2)
                if front:
                    y_stats(3)
                if back:
                    innerT_rest(k, 0)
                    if not last_back:
                        places()
                if front:
                    y_means(3)
                if xn_next:
                    dve.wait_ge(xT_hi, 2 * (s + 2) + 1)
                    turned_rest(xT, tr[0], 0).then_inc(xT_ready, 1)
                if back:
                    innerT_rest(k, 1)
                if front:
                    if back:
                        dve.wait_ge(h2_ready, J * k + J)
                    if xn_next:
                        dve.wait_ge(xn_ready, J * (s + 3))
                    if stats_next:
                        dve.wait_ge(ln1_moments, J * (s + 3) + J)
                    dve.wait_ge(ln2_moments, J * f + J)

                def next_newton(m):
                    if front:
                        newton_op(s + 3, 1 - p, m)

                next_newton(0)
                next_newton(1)
                if back:
                    gated_inner(3)
                next_newton(2)
                if back and not last_back:
                    count()
                next_newton(3)
                if back and not last_back:
                    places_chosen()
                next_newton(4)
                if back:
                    add_shared(k, 0)
                next_newton(5)
                if back and not last_back:
                    slots()
                next_newton(6)
                next_newton(7)

            wait_apart(dve, moments_set, 1)
            def first_stats(b):
                for j in range(J):
                    ln1_stats(b, b, 0, j)
                for j in range(J):
                    ln1_means(b, b, j, b)

            first_stats(0)
            dve.wait_ge(ln1_moments, J)
            for m in range(NEWTON):
                newton_op(0, 0, m)
            dve.wait_ge(attn_w_in, W * 9)
            dve.wait_ge(stage_zeroed, 3)
            parts = [bias_thirds[:, m * 2 * D:(m + 1) * 2 * D] for m in range(3)]
            bias_ops = 1

            def bias_link(ins):
                nonlocal bias_ops
                bias_ops += 1
                ins.then_inc(bias_step, 1)
                dve.wait_ge(bias_step, bias_ops)

            bias_link(dve.tensor_copy(parts[0], bias_f))
            bias_link(dve.tensor_tensor(bias_rest, bias_f, parts[0], ALU.subtract))
            bias_link(dve.tensor_copy(parts[1], bias_rest))
            bias_link(dve.tensor_tensor(bias_rest, bias_rest, parts[1], ALU.subtract))
            bias_link(dve.tensor_copy(parts[2], bias_rest))
            for m in range(3):
                dve.tensor_copy(bias_parts[32 * m:32 * m + 1, :], parts[m][32 * m:32 * m + 1, :]).then_inc(
                    bias_ready, 1)
            dve.wait_ge(attn_hi, 5)
            for (hi, lo), raw in ((wab, raw_wab), (wgd, raw_wgd)):
                dve.tensor_tensor(lo[:], raw.rearrange("q (c n) -> q c n", c=KC), hi[:].bitcast(F32),
                                  ALU.subtract).then_inc(attn_lo, 1)
            dve.tensor_tensor(wc_parts[64:96, :], raw_wc[64:96, :], wc_hi[64:96, :].bitcast(F32),
                              ALU.subtract).then_inc(attn_lo, 1)
            for g in range(2):
                dve.wait_ge(xT_hi, g + 1)
                turned_rest(xT, tr[g], g).then_inc(xT_ready, 1)
            first_stats(1)
            dve.wait_ge(const_ready, 1)
            half_steps(dve, half)

            for e in range(0, E - POOL_SPLITS, 2):
                if e == 2:
                    dve.wait_ge(count_done, 2)
                    dve.tensor_copy(table[:], misc[0:1, :]).then_inc(tab_ready, 1)
                dve.wait_ge(w_hi_ready, e // 2 + 1)
                dve.tensor_tensor(w_lo[:, e:e + 2, :], raw_w[:, e:e + 2, :], w_hi[:, e:e + 2, :].bitcast(F32),
                                  ALU.subtract).then_inc(w_lo_ready, 1)

            def rows_rest(p):
                dve.tensor_tensor(bx[1][:, p, :], tr[p][:], bx[0][:, p, :].bitcast(F32), ALU.subtract).then_inc(bx_lo, 1)

            def results_out(q, w, n):
                p = w % 2
                dve.wait_ge(bdn_done, q + 1)
                if known(n, 1):
                    dve.wait_ge(by_sent[w], 2 * W * n)
                dve.tensor_copy(y[:, w], (gu, dn)[p][:].rearrange("q (h d) -> q h d", h=2)).then_inc(by_ready, 1)

            def pair(q, w, n, last=False):
                p = w % 2
                if not last:
                    dve.wait_ge(bx_hi, q + 2)
                    rows_rest(1 - p)
                dve.wait_ge(bsilu, q + 1)
                if known(q, 2):
                    dve.wait_ge(bth_done, q - 1)
                dve.tensor_tensor(b_inner[:, p, :].rearrange("q (h f) -> q h f", h=2), gu_bank(p)[:, :, F:2 * F],
                                  b_silu[:, p, :].rearrange("q (h f) -> q h f", h=2), ALU.mult).then_inc(binner, 1)
                if known(q, 1):
                    results_out(q - 1, (w + 3) % 4, n if w else n - 1)

            dve.wait_ge(bx_hi, 1)
            rows_rest(0)
            pair(0, 0, 0)
            pair(1, 1, 0)
            for q in range(2, 8):
                pair(q, q % 4, q // 4)
            with dve.Fori(2, PAIRS // 4 - 1) as i:
                for w in range(4):
                    pair(4 * i + w, w, i)
            for q in range(PAIRS - 4, PAIRS):
                pair(q, q % 4, q // 4, last=q == PAIRS - 1)
            results_out(PAIRS - 1, 3, PAIRS // 4 - 1)

            dve.wait_ge(logits_kept, 2 * B)
            dve.tensor_tensor(all_logits[:], all_logits[:], all_best[:, :, 0:1].to_broadcast([P, NT, E]),
                              ALU.subtract).then_inc(prob_step, 1)
            dve.tensor_tensor(prob[:, 1, :], all_best[:, :, 1], all_best[:, :, 0], ALU.subtract).then_inc(prob_step, 1)

            dve.wait_ge(prob_act, 2)
            dve.tensor_reduce(prob[:, 0, :], all_logits[:], AX_X, ALU.add).then_inc(prob_step, 1)
            dve.wait_ge(prob_step, 3)
            dve.reciprocal(prob[:, 0, :], prob[:, 0, :]).then_inc(prob_step, 1)
            dve.wait_ge(prob_step, 4)
            dve.tensor_tensor(prob[:, 1, :], prob[:, 1, :], prob[:, 0, :], ALU.mult).then_inc(prob_step, 1)

            def combine(b, w, n):
                dve.wait_ge(res_in[w], TOP * W * (n + 1))
                for k, done in enumerate((first_added, both_added)):
                    for j in range(J):
                        if k:
                            dve.wait_ge(first_added, J * b + j + 1)
                        tok = tokens[:, J * b + j, :]
                        dve.scalar_tensor_tensor(tok, res[:, w, k, j, :], prob[:, k, bass.ds(J * b + j, 1)], tok,
                                                 ALU.mult, ALU.add).then_inc(done, 1)

            dve.wait_ge(prob_step, 5)
            with dve.Fori(0, B // 4) as i:
                for w in range(4):
                    combine(4 * i + w, w, i)

        @block.gpsimd
        def _(pool):
            steps = 0

            def link(ins):
                nonlocal steps
                steps += 1
                ins.then_inc(const_step, 1)
                wait_apart(pool, const_step, steps)

            link(pool.memset(ident[:], 0.0))
            link(pool.affine_select(out=ident[:], in_=ident[:], compare_op=ALU.not_equal, fill=1.0, base=0,
                                    pattern=[[-1, P]], channel_multiplier=1))
            link(pool.memset(ones[:], 1.0))
            link(pool.affine_select(out=earlier[:], in_=ones[:], compare_op=ALU.is_gt, fill=0.0, base=0,
                                    pattern=[[1, P]], channel_multiplier=-1))
            link(pool.memset(chosen_sum[:], 0.0))
            link(pool.memset(fill_rows[:, 0:D], 0.0))
            link(pool.memset(fill_rows[:, D:ROW].bitcast(I32), NOWHERE))
            link(pool.memset(ones_row[:], 1.0))
            link(pool.iota(tile_no_i[:], pattern=[[P, 2]], base=0, channel_multiplier=1))
            link(pool.tensor_copy(tile_no[:], tile_no_i[:]))
            link(pool.memset(row_buf[:, :, :, D:ROW], 0.0))
            it = slot[:].rearrange("q a k j -> q (a k j)")
            assert E <= 2 * TOP * J
            link(pool.iota(it[:, 0:E], pattern=[[1, E]], base=0, channel_multiplier=0))
            link(pool.tensor_copy(expert_of_col[:], it[:, 0:E]))
            for j in range(J):
                link(pool.tensor_scalar(region_of_col[:, j, :], expert_of_col[:], float(REGION), None, ALU.mult))
            pool.iota(result_row[:], pattern=[[P, J]], base=0, channel_multiplier=1).then_inc(const_ready, 1)

            wait_apart(pool, ffn_hi, 3)
            for (hi, lo), raw in ((wsh, raw_wsh), (wshd, raw_wshd)):
                pool.tensor_tensor(lo[:], raw.rearrange("q (c n) -> q c n", c=KC), hi[:].bitcast(F32),
                                   ALU.subtract).then_inc(ffn_lo, 1)
            pool.tensor_tensor(wrt[:, :, E:2 * E], raw_wrt.rearrange("q (c n) -> q c n", c=KC), wrt[:, :, 0:E].bitcast(F32),
                               ALU.subtract).then_inc(ffn_lo, 1)

            def half(s, p, n=0):
                f, k = s + 1, s
                front, back, tail = has_front(s), has_back(s), known(s, 1)
                n_tail = (s - 1) // 2 if isinstance(s, int) else n - 1 + p

                def x_plus_dx(j):
                    wait_apart(pool, dx_ready, J * f + j + 1)
                    if known(f, 1) or j >= 2:
                        wait_apart(pool, x1_ready, J * f + j - 1)
                    pool.tensor_tensor(xdx[:, j % 2, :], tokens[:, J * f + j, :], dx[:, j % 2, :],
                                       ALU.add).then_inc(xdx_ready, 1)

                def send(q, choice, j, done):
                    pool.indirect_dma_start(
                        out=rows, out_offset=bass.IndirectOffsetOnAxis(ap=slot[:, q, choice, j:j + 1], axis=0),
                        in_=row_buf[:, q, j, :], in_offset=None).then_inc(done, W)

                if back:
                    if known(k, 2):
                        wait_apart(pool, sent2[p], W * J * n)
                    if known(k, 1):
                        wait_apart(pool, result_row_ready, k)
                    pool.tensor_copy(row_buf[:, p, :, D].bitcast(I32), result_row[:]).then_inc(first_id, 1)
                    wait_apart(pool, first_id, k + 1)
                    pool.tensor_scalar(result_row[:], result_row[:], S, None, ALU.add).then_inc(result_row_ready, 1)
                if tail:
                    wait_apart(pool, sent1[1 - p], W * J * (n_tail + 1))
                    wait_apart(pool, t2_done, 2 * k)
                    pool.tensor_scalar(row_buf[:, 1 - p, :, D].bitcast(I32), row_buf[:, 1 - p, :, D].bitcast(I32), T, None,
                                       ALU.add).then_inc(second_id, 1)
                if front:
                    x_plus_dx(0)
                if tail:
                    wait_apart(pool, second_id, k)
                    send(1 - p, 1, 0, sent2[1 - p])
                    send(1 - p, 1, 1, sent2[1 - p])
                if front:
                    x_plus_dx(1)
                if tail:
                    send(1 - p, 1, 2, sent2[1 - p])
                if front:
                    x_plus_dx(2)
                if tail:
                    send(1 - p, 1, 3, sent2[1 - p])
                if back:
                    wait_apart(pool, logits_ready, k + 1)
                    pool.tensor_copy(all_logits[:, bass.ds(J * k, J), :], logits[:]).then_inc(logits_kept, 1)
                    wait_apart(pool, best_at_ready, J * k + J)
                    pool.tensor_copy(all_best[:, bass.ds(J * k, J), :], best[:, :, 0:TOP]).then_inc(logits_kept, 1)
                if front:
                    x_plus_dx(3)
                if back:
                    wait_apart(pool, slot_ready, k + 1)
                    wait_apart(pool, h2_ready, J * k + J)
                    wait_apart(pool, first_id, k + 1)
                    for j in range(J):
                        send(p, 0, j, sent1[p])

            half_steps(pool, half)

            wait_apart(pool, w_hi_ready, E // 2)
            wait_apart(pool, shared_added, J * B)
            for e in range(E - POOL_SPLITS, E, 2):
                pool.tensor_tensor(w_lo[:, e:e + 2, :], raw_w[:, e:e + 2, :], w_hi[:, e:e + 2, :].bitcast(F32),
                                   ALU.subtract).then_inc(w_lo_ready, 1)

            def keep_ids(q, w, n, at):
                wait_apart(pool, bt_done, q + 1)
                if known(q, 8):
                    wait_apart(pool, by_sent[w], 2 * W * (n - 1))
                pool.tensor_copy(row_ids[:, at, :], row_buf[:, w // 2, 2 * (w % 2):2 * (w % 2) + 2, D].bitcast(I32)).then_inc(
                    ids_kept, 1)

            def send_pair(q, w, at):
                wait_apart(pool, by_ready, q + 1)
                wait_apart(pool, ids_kept, q + 1)
                for h in range(2):
                    pool.indirect_dma_start(
                        out=results, out_offset=bass.IndirectOffsetOnAxis(ap=row_ids[:, at, h:h + 1], axis=0),
                        in_=y[:, w, h, :], in_offset=None, bounds_check=TOP * T - 1,
                        oob_is_err=False).then_inc(by_sent[w], W)

            AHEAD = 4
            assert PAIRS % 8 == 0
            for q in range(AHEAD):
                keep_ids(q, q, 0, q)
            for q in range(8):
                keep_ids(q + AHEAD, q % 4, q // 4 + 1, (q + AHEAD) % 8)
                send_pair(q, q % 4, q)
            with pool.Fori(1, PAIRS // 8 - 1) as i:
                for m in range(8):
                    keep_ids(8 * i + m + AHEAD, m % 4, 2 * i + m // 4 + 1, (m + AHEAD) % 8)
                    send_pair(8 * i + m, m % 4, m)
            for q in range(PAIRS - 8, PAIRS):
                if q + AHEAD < PAIRS:
                    keep_ids(q + AHEAD, q % 4, q // 4 + 1, (q + AHEAD) % 8)
                send_pair(q, q % 4, q % 8)


def kernel(**inputs):
    import numpy as _np
    import concourse.bacc as _bacc
    from concourse import mybir as _mybir
    from concourse.bass_utils import run_bass_kernel_spmd as _run

    a = {k: _np.asarray(v) for k, v in inputs.items()}
    laid = {
        "x": a["L0_attn_x"],
        "wa_t": a["L0_attn_WA"].T,
        "wb_t": a["L0_attn_WB"].T,
        "wc_t": a["L0_attn_WC"].T,
        "wgd_t": _np.concatenate([a["L0_attn_Wg"].T, a["L0_attn_WD"].T], axis=1),
        "bias": _np.concatenate([a["L0_attn_bg"], a["L0_attn_bD"]])[None],
        "router_w": a["L0_ffn_router_w"],
        "gate_w": a["L0_ffn_gate_w"],
        "up_w": a["L0_ffn_up_w"],
        "down_w": a["L0_ffn_down_w"],
        "shared_gu": _np.concatenate([a["L0_ffn_shared_gate_w"], a["L0_ffn_shared_up_w"]], axis=1),
        "shared_down": a["L0_ffn_shared_down_w"],
    }
    nc = _bacc.Bacc("TRN2", target_bir_lowering=False, num_devices=1)
    arrays, args = {}, []
    for name, v in laid.items():
        v = _np.ascontiguousarray(v)
        arrays[f"in_{name}"] = v
        args.append(nc.dram_tensor(f"in_{name}", v.shape, _mybir.dt.from_np(v.dtype), kind="ExternalInput").ap())
    args.append(nc.dram_tensor("out_0", laid["x"].shape, _mybir.dt.float32, kind="ExternalOutput").ap())
    preln_gated_scan_and_routed_experts(nc, *args)
    r = _run(nc, [arrays], core_ids=[0])
    return r.results[0]["out_0"]
```
